# Optimizing a Trainium2 kernel written in Bass

```python
import numpy as np
import jax
import jax.numpy as jnp

def _softmax(x, axis=-1):
    return jax.nn.softmax(x, axis=axis)

def _gelu(x):
    return jax.nn.gelu(x, approximate=True)

def _silu(x):
    return jax.nn.silu(x)

def _sigmoid(x):
    return jax.nn.sigmoid(x)

def _layernorm(x, axis=-1, eps=1e-05):
    m = jnp.mean(x, axis=axis, keepdims=True)
    v = jnp.var(x, axis=axis, keepdims=True)
    return (x - m) / jnp.sqrt(v + eps)

def _scatter_add(tgt, idx, src, axis=0):
    return tgt.at[idx].add(src)

def _segment_sum(src, seg, n):
    return jax.ops.segment_sum(src, seg, n)
kernel_name = 'mk_adj_resnorm_d4_adj_r2_5864fe'

def setup_inputs(seed: int=0):
    np.random.seed(seed)
    _w = jnp.asarray

    def _rec_inputs():
        import jax
        import jax.numpy as jnp
        _gk = jax.random.key(seed)
        x = 7.22e-05 + 1 * jax.random.normal(jax.random.fold_in(_gk, 1), (32, 256, 256), jnp.float32)
        _a = jax.random.bernoulli(jax.random.fold_in(_gk, 2), 0.015625, (256, 256))
        _a = jnp.logical_or(_a, jnp.swapaxes(_a, -1, -2))
        _a = jnp.logical_or(_a, jnp.eye(256, dtype=bool))
        _af = _a.astype(jnp.float32)
        _af = _af * jax.random.uniform(jax.random.fold_in(_gk, 3), (256, 256), jnp.float32, 0.05, 0.00390622)
        adj = _af
        return (x, adj)
    x, adj = _rec_inputs()

    def _L0_gnn_setup():
        import jax, jax.numpy as jnp
        import numpy as np
        B, N, D, T = (64, 128, 256, 3)

        def _lin(v, W, b):
            return jnp.einsum('...i,oi->...o', v, W) + b
        key = jax.random.key(seed)
        ks = jax.random.split(key, 12)
        s2 = 1.0 / np.sqrt(2 * D)
        s1 = 1.0 / np.sqrt(D)
        return {'x': jax.random.normal(ks[0], (B, N, D), jnp.float32), 'in_mat': jax.random.uniform(ks[1], (N, N), jnp.float32) / N, 'out_mat': jax.random.uniform(ks[2], (N, N), jnp.float32) / N, 'w3_w': jax.random.normal(ks[3], (D, 2 * D), jnp.float32) * s2, 'w3_b': jnp.zeros((D,), jnp.float32), 'u3_w': jax.random.normal(ks[4], (D, D), jnp.float32) * s1, 'u3_b': jnp.zeros((D,), jnp.float32), 'w4_w': jax.random.normal(ks[5], (D, 2 * D), jnp.float32) * s2, 'w4_b': jnp.zeros((D,), jnp.float32), 'w5_w': jax.random.normal(ks[6], (D, 2 * D), jnp.float32) * s2, 'w5_b': jnp.zeros((D,), jnp.float32), 'u5_w': jax.random.normal(ks[7], (D, D), jnp.float32) * s1, 'u5_b': jnp.zeros((D,), jnp.float32)}
    _L0_gnn_all = _L0_gnn_setup()
    _L0_gnn_in = {k: v for k, v in _L0_gnn_all.items() if k in ('w3_w', 'w3_b', 'u3_w', 'u3_b', 'w4_w', 'w4_b', 'w5_w', 'w5_b', 'u5_w', 'u5_b')}
    del _L0_gnn_all

    def _L1_gnn_setup():
        import jax, jax.numpy as jnp
        import numpy as np
        B, N, D = (8, 1024, 256)
        key = jax.random.key(seed)
        k1, k2, k3, k4, k5 = jax.random.split(key, 5)
        neuron_states = jax.random.normal(k1, (B, N, D), dtype=jnp.float32)
        adjacency = jax.random.randint(k2, (N, N), 0, 2).astype(jnp.float32)
        scale = 1.0 / np.sqrt(D)
        Wq = jax.random.normal(k3, (D, D), dtype=jnp.float32) * scale
        Wk = jax.random.normal(k4, (D, D), dtype=jnp.float32) * scale
        Wv = jax.random.normal(k5, (D, D), dtype=jnp.float32) * scale
        return {'neuron_states': neuron_states, 'adjacency': adjacency, 'Wq': Wq, 'Wk': Wk, 'Wv': Wv}
    _L1_gnn_all = _L1_gnn_setup()
    _L1_gnn_in = {k: v for k, v in _L1_gnn_all.items() if k in ('Wq', 'Wk', 'Wv')}
    del _L1_gnn_all

    def _L2_gnn_setup():
        import jax, jax.numpy as jnp
        import numpy as np
        B, N, D, O = (8, 2048, 256, 256)
        key = jax.random.key(seed)
        k1, k2, k3, k4 = jax.random.split(key, 4)
        x = jax.random.normal(k1, (B, N, D), dtype=jnp.float32)
        adj = jax.random.uniform(k2, (N, N), dtype=jnp.float32)
        weight = jax.random.normal(k3, (D, O), dtype=jnp.float32) * 0.02
        bias = jax.random.normal(k4, (O,), dtype=jnp.float32) * 0.02
        return {'x': x, 'adj': adj, 'weight': weight, 'bias': bias}
    _L2_gnn_all = _L2_gnn_setup()
    _L2_gnn_in = {k: v for k, v in _L2_gnn_all.items() if k in ('weight', 'bias')}
    del _L2_gnn_all

    def _L3_gnn_setup():
        import jax, jax.numpy as jnp
        import numpy as np
        B, N, F_IN, F_OUT = (16, 1024, 256, 256)
        key = jax.random.key(seed)
        k1, k2, k3 = jax.random.split(key, 3)
        x = jax.random.normal(k1, (B, N, F_IN), dtype=jnp.float32)
        adj = jax.random.uniform(k2, (N, N), dtype=jnp.float32)
        bound = np.sqrt(6.0 / F_OUT)
        weight = jax.random.uniform(k3, (F_IN, F_OUT), dtype=jnp.float32, minval=-bound, maxval=bound)
        bias = jnp.zeros((F_OUT,), dtype=jnp.float32)
        return {'x': x, 'adj': adj, 'weight': weight, 'bias': bias}
    _L3_gnn_all = _L3_gnn_setup()
    _L3_gnn_in = {k: v for k, v in _L3_gnn_all.items() if k in ('weight', 'bias')}
    del _L3_gnn_all
    return {'x': x, 'adj': adj, 'L0_gnn_w3_w': _L0_gnn_in['w3_w'], 'L0_gnn_w3_b': _L0_gnn_in['w3_b'], 'L0_gnn_u3_w': _L0_gnn_in['u3_w'], 'L0_gnn_u3_b': _L0_gnn_in['u3_b'], 'L0_gnn_w4_w': _L0_gnn_in['w4_w'], 'L0_gnn_w4_b': _L0_gnn_in['w4_b'], 'L0_gnn_w5_w': _L0_gnn_in['w5_w'], 'L0_gnn_w5_b': _L0_gnn_in['w5_b'], 'L0_gnn_u5_w': _L0_gnn_in['u5_w'], 'L0_gnn_u5_b': _L0_gnn_in['u5_b'], 'L1_gnn_Wq': _L1_gnn_in['Wq'], 'L1_gnn_Wk': _L1_gnn_in['Wk'], 'L1_gnn_Wv': _L1_gnn_in['Wv'], 'L2_gnn_weight': _L2_gnn_in['weight'], 'L2_gnn_bias': _L2_gnn_in['bias'], 'L3_gnn_weight': _L3_gnn_in['weight'], 'L3_gnn_bias': _L3_gnn_in['bias']}

def reference(x, adj, L0_gnn_w3_w, L0_gnn_w3_b, L0_gnn_u3_w, L0_gnn_u3_b, L0_gnn_w4_w, L0_gnn_w4_b, L0_gnn_w5_w, L0_gnn_w5_b, L0_gnn_u5_w, L0_gnn_u5_b, L1_gnn_Wq, L1_gnn_Wk, L1_gnn_Wv, L2_gnn_weight, L2_gnn_bias, L3_gnn_weight, L3_gnn_bias):
    import jax
    import jax.numpy as jnp

    def _L0_gnn_ref(x, in_mat, out_mat, w3_w, w3_b, u3_w, u3_b, w4_w, w4_b, w5_w, w5_b, u5_w, u5_b):
        import jax, jax.numpy as jnp
        import numpy as np
        B, N, D, T = (64, 128, 256, 3)

        def _lin(v, W, b):
            return jnp.einsum('...i,oi->...o', v, W) + b
        h = x
        for _ in range(T):
            a_in = jnp.einsum('nm,bmd->bnd', in_mat, h)
            a_out = jnp.einsum('nm,bmd->bnd', out_mat, h)
            av = jnp.concatenate([a_in, a_out], axis=-1)
            z = jax.nn.sigmoid(_lin(av, w3_w, w3_b) + _lin(h, u3_w, u3_b))
            r = jax.nn.sigmoid(_lin(av, w4_w, w4_b) + _lin(h, u3_w, u3_b))
            hv = jnp.tanh(_lin(av, w5_w, w5_b) + _lin(r * h, u5_w, u5_b))
            h = (1.0 - z) * h + z * hv
        return h

    def _L1_gnn_ref(neuron_states, adjacency, Wq, Wk, Wv):
        import jax, jax.numpy as jnp
        import numpy as np
        B, N, D = (8, 1024, 256)
        q = jnp.einsum('bnd,ed->bne', neuron_states, Wq)
        k = jnp.einsum('bnd,ed->bne', neuron_states, Wk)
        v = jnp.einsum('bnd,ed->bne', neuron_states, Wv)
        rel = jnp.einsum('bnd,bmd->bnm', q, k)
        rel = adjacency.T[None, :, :] * rel
        rel = rel / jnp.linalg.norm(rel, axis=2, keepdims=True)
        return jnp.einsum('bnm,bmd->bnd', rel, v)

    def _L2_gnn_ref(x, adj, weight, bias):
        import jax, jax.numpy as jnp
        import numpy as np
        B, N, D, O = (8, 2048, 256, 256)
        y = jnp.einsum('nm,bmd->bnd', adj, x)
        out = jnp.einsum('bnd,do->bno', y, weight) + bias
        return out

    def _L3_gnn_ref(x, adj, weight, bias):
        import jax, jax.numpy as jnp
        import numpy as np
        B, N, F_IN, F_OUT = (16, 1024, 256, 256)
        deg = adj.sum(axis=1)
        deg_inv_sqrt = jnp.where(deg > 0, jax.lax.rsqrt(deg), 0.0)
        norm_adj = adj * deg_inv_sqrt[:, None] * deg_inv_sqrt[None, :]
        support = jnp.einsum('bni,io->bno', x, weight)
        output = jnp.einsum('nm,bmo->bno', norm_adj, support)
        return output + bias
    x = _layernorm(x + _L0_gnn_ref(x, adj, adj, L0_gnn_w3_w, L0_gnn_w3_b, L0_gnn_u3_w, L0_gnn_u3_b, L0_gnn_w4_w, L0_gnn_w4_b, L0_gnn_w5_w, L0_gnn_w5_b, L0_gnn_u5_w, L0_gnn_u5_b), axis=-1)
    x = _layernorm(x + _L1_gnn_ref(x, adj, L1_gnn_Wq, L1_gnn_Wk, L1_gnn_Wv), axis=-1)
    x = _layernorm(x + _L2_gnn_ref(x, adj, L2_gnn_weight, L2_gnn_bias), axis=-1)
    x = _layernorm(x + _L3_gnn_ref(x, adj, L3_gnn_weight, L3_gnn_bias), axis=-1)
    return x

_drawn_inputs = setup_inputs


def setup_inputs(seed=0):
    import zlib

    import numpy as np

    out = dict(_drawn_inputs(seed))
    spreads = {'L0_gnn_w3_b': (0.0, 0.308),
     'L0_gnn_u3_b': (0.0, 0.274),
     'L0_gnn_w4_b': (0.0, 0.662),
     'L0_gnn_w5_b': (0.0, 0.1),
     'L0_gnn_u5_b': (0.0, 0.1),
     'L3_gnn_bias': (0.0, 0.1)}
    factors = {'L0_gnn_w4_w': 4.698}
    for name, (base, spread) in spreads.items():
        noise = np.random.default_rng([zlib.crc32(name.encode()), seed]).standard_normal(out[name].shape)
        drawn = base * np.exp(spread * noise) if base else spread * noise
        out[name] = jnp.asarray(drawn.astype(out[name].dtype))
    for name, factor in factors.items():
        out[name] = (out[name] * factor).astype(out[name].dtype)
    return out
```

```python
from contextlib import ExitStack

import concourse.bass as bass
from concourse import mybir

P = 128
F32 = mybir.dt.float32
F32R = mybir.dt.float32r
ALU = mybir.AluOpType
ACT = mybir.ActivationFunctionType
AX = mybir.AxisListType
EPS = 1e-5
TINY = 1.1754944e-38


class Split:

    def __init__(self, hi, lo):
        self.hi, self.lo = hi, lo


class State:

    def __init__(self, sb, sem, name, full, by_graph):
        self.feat = sb(f"{name}_feat", full)
        self.feat_hi, self.feat_lo = sb(f"{name}_feat_hi", full, F32R), sb(f"{name}_feat_lo", full, F32R)
        self.node_hi, self.node_lo = sb(f"{name}_node_hi", by_graph, F32R), sb(f"{name}_node_lo", by_graph, F32R)
        self.s_feat = sem(f"{name}_s_feat")
        self.s_feat_hi, self.s_feat_lo = sem(f"{name}_s_feat_hi"), sem(f"{name}_s_feat_lo")
        self.s_turned = sem(f"{name}_s_turned")
        self.s_node_hi, self.s_node_lo = sem(f"{name}_s_node_hi"), sem(f"{name}_s_node_lo")


class Lane:

    def __init__(self, sb, psum, sem, name, state, full):
        self.state = state
        self.ps0, self.ps1 = psum(f"{name}_ps0", full), psum(f"{name}_ps1", full)
        self.a_hi, self.a_lo = sb(f"{name}_a_hi", full, F32R), sb(f"{name}_a_lo", full, F32R)
        self.gate = sb(f"{name}_gate", full)
        self.rh_hi, self.rh_lo = sb(f"{name}_rh_hi", full, F32R), sb(f"{name}_rh_lo", full, F32R)
        self.z = sb(f"{name}_z", full)
        self.kept = sb(f"{name}_kept", full)
        self.cand = sb(f"{name}_cand", full)
        self.s_mixed = sem("{}_s_mixed".format(name))
        self.s_a_hi = sem("{}_s_a_hi".format(name))
        self.s_a_lo = sem("{}_s_a_lo".format(name))
        self.s_base = sem("{}_s_base".format(name))
        self.s_base_kept = sem("{}_s_base_kept".format(name))
        self.s_reset = sem("{}_s_reset".format(name))
        self.s_reset_arg = sem("{}_s_reset_arg".format(name))
        self.s_r = sem("{}_s_r".format(name))
        self.s_rh = sem("{}_s_rh".format(name))
        self.s_rh_hi = sem("{}_s_rh_hi".format(name))
        self.s_rh_lo = sem("{}_s_rh_lo".format(name))
        self.s_update = sem("{}_s_update".format(name))
        self.s_z = sem("{}_s_z".format(name))
        self.s_zh = sem("{}_s_zh".format(name))
        self.s_kept = sem("{}_s_kept".format(name))
        self.s_cand = sem("{}_s_cand".format(name))
        self.s_tanh = sem("{}_s_tanh".format(name))
        self.s_zc = sem("{}_s_zc".format(name))


def build(nc, x, adj, w3_w, w3_b, u3_w, u3_b, w4_w, w4_b, w5_w, w5_b, u5_w, u5_b, wq, wk, wv,
          l2_w, l2_b, l3_w, l3_b, out):
    B, N, D = x.shape
    C = N // P
    G = 2
    T = G * N
    PAIRS = B // G
    assert N == D and C == 2 and T == 512
    LAST = PAIRS - 1

    x_pairs = x.rearrange("(q g) (c p) d -> q p g c d", g=G, p=P)
    out_pairs = out.rearrange("(q g) (c p) d -> q p g c d", g=G, p=P)

    with ExitStack() as ctx:
        def sb(name, shape, dt=F32):
            return ctx.enter_context(nc.sbuf_tensor(name, shape, dt))

        def sem(name):
            return ctx.enter_context(nc.semaphore(name))

        def split_matrix(name):
            return Split(sb(name + "_hi", [P, C, D], F32R), sb(name + "_lo", [P, C, D], F32R))

        adjT = split_matrix("adjT")
        norm_adjT = split_matrix("norm_adjT")
        w3T = split_matrix("w3T")
        w4T = split_matrix("w4T")
        w5T = split_matrix("w5T")
        u3T = split_matrix("u3T")
        u5T = split_matrix("u5T")
        wvT = split_matrix("wvT")
        wqk = split_matrix("wqk")
        w2s = split_matrix("w2s")
        w3s = split_matrix("w3s")

        ident = sb("ident", [P, P])
        adj_nat = sb("adj_nat", [P, C, N])
        ones = sb("ones", [P, 1])
        neg_half = sb("neg_half", [P, 2 * C])
        bias_in = sb("bias_in", [P, 5, C])
        bias_z = sb("bias_z", [P, C])
        bias_r = sb("bias_r", [P, C])
        bias_c = sb("bias_c", [P, C])
        bias_out = sb("bias_out", [P, 2, D])
        deg = sb("deg", [P, C])
        deg_floor = sb("deg_floor", [P, C])
        deg_pos = sb("deg_pos", [P, C])
        deg_pow = sb("deg_pow", [P, C])
        deg_inv = sb("deg_inv", [P, C])

        def psum(name, shape):
            return ctx.enter_context(nc.psum_tensor(name, shape, F32))

        state_f = State(sb, sem, "hf", [P, C, T], [P, G, C, D])
        state_b = State(sb, sem, "hb", [P, C, T], [P, G, C, D])
        front = Lane(sb, psum, sem, "f", state_f, [P, C, T])
        back = Lane(sb, psum, sem, "b", state_b, [P, C, T])

        def per_graph(t):
            return t[:].rearrange("p c (k n) -> p c k n", k=C)

        x_front = sb("x_front", [P, G, C, D])
        x_back = sb("x_back", [P, G, C, D])
        h3 = back.cand
        summed = sb("summed", [P, G, C, D])
        normed = sb("normed", [P, G, C, D])
        skip = sb("skip", [P, G, C, D])
        result = sb("result", [P, G, C, D])
        x_hi, x_lo = per_graph(back.a_hi), per_graph(back.a_lo)
        y_hi, y_lo = per_graph(back.rh_hi), per_graph(back.rh_lo)
        v_hi, v_lo = sb("v_hi", [P, G, C, D], F32R), sb("v_lo", [P, G, C, D], F32R)
        rel, rel_sq = per_graph(back.gate), per_graph(back.z)
        rel_hi, rel_lo = sb("rel_hi", [P, G, C, N], F32R), sb("rel_lo", [P, G, C, N], F32R)
        stats = sb("stats", [P, G, C, 6])
        moments = sb("moments", [P, G, C, 2])
        pad = sb("pad", [P, 1])
        var_eps = sb("var_eps", [P, G, C])
        rstd = sb("rstd", [P, G, C])
        norm_sq = sb("norm_sq", [P, G, C])
        norm_inv = sb("norm_inv", [P, G, C])

        w3_nat, w4_nat, w5_nat = back.gate[:], back.z[:], back.kept[:]
        flat = lambda t: t[:].rearrange("p g c d -> p (g c) d")
        u3_nat, u5_nat = flat(x_back)[:, 0:C], flat(x_back)[:, C:2 * C]
        wq_nat, wk_nat = flat(summed)[:, 0:C], flat(summed)[:, C:2 * C]
        wv_nat, w2_nat = flat(normed)[:, 0:C], flat(normed)[:, C:2 * C]
        w3s_nat = flat(skip)[:, 0:C]
        adj_rows, norm_full = flat(result)[:, 0:C], flat(result)[:, C:2 * C]

        s_x_front, s_x_back, s_stored = sem("s_x_front"), sem("s_x_back"), sem("s_stored")
        s_load = {n: sem("s_load_" + n) for n in ("adj", "u3", "w4", "w3", "w5", "u5", "qk", "v", "l23", "bias")}
        s_consts, s_bias, s_halves = sem("s_consts"), sem("s_bias"), sem("s_halves")
        s_deg, s_deg_pow, s_rows, s_norm_full = sem("s_deg"), sem("s_deg_pow"), sem("s_rows"), sem("s_norm_full")
        s_prep, s_prep_hi, s_prep_lo = sem("s_prep"), sem("s_prep_hi"), sem("s_prep_lo")
        s_in_turned = sem("s_in_turned")
        s_h3, s_h3_turned = sem("s_h3"), sem("s_h3_turned")
        s_sum, s_stats, s_moments, s_var, s_rstd, s_normed = (
            sem("s_sum"), sem("s_stats"), sem("s_moments"), sem("s_var"), sem("s_rstd"), sem("s_normed"))
        s_x1_turned, s_x1_hi, s_x1_lo = sem("s_x1_turned"), sem("s_x1_hi"), sem("s_x1_lo")
        s_y, s_y_hi, s_y_lo = sem("s_y"), sem("s_y_hi"), sem("s_y_lo")
        s_v, s_v_hi, s_v_lo = sem("s_v"), sem("s_v_hi"), sem("s_v_lo")
        s_rel, s_masked, s_rel_hi, s_rel_sq, s_rel_lo = (
            sem("s_rel"), sem("s_masked"), sem("s_rel_hi"), sem("s_rel_sq"), sem("s_rel_lo"))
        s_norm, s_norm_sq, s_norm_inv, s_attended = sem("s_norm"), sem("s_norm_sq"), sem("s_norm_inv"), sem("s_attended")
        s_x_hi, s_x_lo, s_skip = sem("s_x_hi"), sem("s_x_lo"), sem("s_skip")
        s_ax, s_ax_hi, s_ax_lo, s_conv = sem("s_ax"), sem("s_ax_hi"), sem("s_ax_lo"), sem("s_conv")

        def upto(n, k=1):
            return 2 * n + k + 1

        def ln(q, j, g):
            return 8 * q + 2 * j + g + 1

        def conv(q, j, g=1):
            return 4 * q + 2 * j + g + 1

        prepared = [adjT, u3T, w4T, w3T, w5T, u5T, wvT, wqk, norm_adjT]

        def prep_bank(i):
            ps = (back.ps0, back.ps1)[i // 2 % 2]
            return ps[:, i % 2, :].rearrange("p (c n) -> p c n", c=C)

        def later(n):
            return not (isinstance(n, int) and n == 0)

        block = ctx.enter_context(nc.Block())

        @block.sync
        def _(sp):
            def rows(w):
                return w.rearrange("(c p) d -> p c d", p=P)

            sp.dma_start(adj_nat[:], rows(adj)).then_inc(s_load["adj"], 16)
            sp.dma_start(x_front[:], x_pairs[0]).then_inc(s_x_front, 16)
            sp.dma_start(u3_nat, rows(u3_w)).then_inc(s_load["u3"], 16)
            sp.dma_start(w4_nat, rows(w4_w)).then_inc(s_load["w4"], 16)
            sp.dma_start(w3_nat, rows(w3_w)).then_inc(s_load["w3"], 16)
            sp.dma_start(w5_nat, rows(w5_w)).then_inc(s_load["w5"], 16)
            sp.dma_start(u5_nat, rows(u5_w)).then_inc(s_load["u5"], 16)
            sp.dma_start(wv_nat, rows(wv)).then_inc(s_load["v"], 16)
            sp.dma_start(wq_nat, rows(wq)).then_inc(s_load["qk"], 16)
            sp.dma_start(wk_nat, rows(wk)).then_inc(s_load["qk"], 16)
            sp.dma_start(w2_nat, rows(l2_w)).then_inc(s_load["l23"], 16)
            sp.dma_start(w3s_nat, rows(l3_w)).then_inc(s_load["l23"], 16)

            def load_front(p):
                sp.wait_ge(s_in_turned, upto(p - 1))
                sp.wait_ge(state_f.s_node_lo, upto(2 * p - 2))
                sp.dma_start(x_front[:], x_pairs[p]).then_inc(s_x_front, 16)

            def load_back(q):
                sp.wait_ge(s_sum, ln(q - 1, 0, 1))
                sp.dma_start(x_back[:], x_pairs[q]).then_inc(s_x_back, 16)

            def store(q):
                sp.wait_ge(s_normed, ln(q, 3, 1))
                sp.dma_start(out_pairs[q], result[:]).then_inc(s_stored, 16)

            load_front(1)
            sp.wait_ge(s_prep, 6)
            sp.dma_start(x_back[:], x_pairs[0]).then_inc(s_x_back, 16)
            with sp.Fori(1, LAST) as p:
                load_front(p + 1)
                load_back(p)
                store(p - 1)
            load_back(LAST)
            store(LAST - 1)
            store(LAST)
            sp.wait_ge(s_stored, 16 * PAIRS)

        @block.gpsimd
        def _(pool):
            pool.memset(ident[:], 0.0).then_inc(s_consts, 1)
            pool.memset(ones[:], 1.0).then_inc(s_consts, 1)
            pool.memset(neg_half[:], -0.5).then_inc(s_consts, 1)
            pool.wait_ge(s_consts, 3)
            pool.affine_select(out=ident[:], in_=ident[:], compare_op=ALU.not_equal, fill=1.0, base=0,
                               pattern=[[-1, P]], channel_multiplier=1).then_inc(s_consts, 1)
            for i, b in enumerate((w3_b, u3_b, w4_b, w5_b, u5_b)):
                pool.dma_start(bias_in[:, i, :], b.rearrange("(c p) -> p c", p=P),
                               allow_slow_non_contiguous=True).then_inc(s_load["bias"], 16)
            for i, b in enumerate((l2_b, l3_b)):
                pool.dma_start(bias_out[:, i, :], b.partition_broadcast(P)).then_inc(s_load["bias"], 16)

            pool.wait_ge(s_deg, 3)
            pool.tensor_tensor(deg_pow[:], deg_floor[:], neg_half[:, 0:C], ALU.pow).then_inc(s_deg_pow, 1)

            def keep(L, n):
                S = L.state
                pool.wait_ge(S.s_feat, upto(n))
                for k in range(C):
                    pool.wait_ge(L.s_z, upto(n, k))
                    pool.tensor_tensor(L.kept[:, k], L.z[:, k], S.feat[:, k], ALU.mult).then_inc(L.s_zh, 1)
                for k in range(C):
                    pool.wait_ge(L.s_zh, upto(n, k))
                    pool.tensor_tensor(L.kept[:, k], S.feat[:, k], L.kept[:, k], ALU.subtract).then_inc(L.s_kept, 1)

            def inverse_std(q, j, g):
                pool.wait_ge(s_var, ln(q, j, g))
                pool.tensor_tensor(rstd[:, g], var_eps[:, g], neg_half[:, 0:C], ALU.pow).then_inc(s_rstd, 1)

            def inverse_norm(q):
                pool.wait_ge(s_norm_sq, q + 1)
                pool.tensor_tensor(norm_inv[:].rearrange("p g c -> p (g c)"), norm_sq[:].rearrange("p g c -> p (g c)"),
                                   neg_half[:], ALU.pow).then_inc(s_norm_inv, 1)

            def add_bias(q, j, g):
                pool.wait_ge(s_normed, ln(q, j + 1, g))
                for c in range(C):
                    ins = pool.tensor_tensor(skip[:, g, c], normed[:, g, c], bias_out[:, j], ALU.add)
                ins.then_inc(s_skip, 1)

            def body(p, q):
                if q is not None:
                    keep(back, q)
                if p is not None:
                    keep(front, 2 * p)
                if q is not None:
                    for g in range(G):
                        inverse_std(q, 0, g)
                    inverse_norm(q)
                    for g in range(G):
                        inverse_std(q, 1, g)
                    for g in range(G):
                        add_bias(q, 0, g)
                if p is not None:
                    keep(front, 2 * p + 1)
                if q is not None:
                    for g in range(G):
                        inverse_std(q, 2, g)
                    for g in range(G):
                        add_bias(q, 1, g)
                    for g in range(G):
                        inverse_std(q, 3, g)

            pool.wait_ge(s_load["bias"], 16 * 7)
            body(0, None)
            body(1, 0)
            with pool.Fori(2, PAIRS) as p:
                body(p, p - 1)
            body(None, LAST)

        @block.tensor
        def _(pe):
            def product(bank, stationary, moving, start=True, stop=True):
                terms = [(s, m) for (sh, sl), (mh, ml) in zip(stationary, moving)
                         for s, m in ((sh, mh), (sh, ml), (sl, mh))]
                for i, (s, m) in enumerate(terms):
                    last = pe.matmul(bank, s, m, start=start and i == 0, stop=stop and i == len(terms) - 1,
                                     skip_group_check=True)
                return last

            def columns(m, k):
                return [(m.hi[:, c, k * P:(k + 1) * P], m.lo[:, c, k * P:(k + 1) * P]) for c in range(C)]

            def whole(m):
                return [(m.hi[:, c, :], m.lo[:, c, :]) for c in range(C)]

            def graph_columns(hi, lo, g, k):
                return [(hi[:, g, c, k * P:(k + 1) * P], lo[:, g, c, k * P:(k + 1) * P]) for c in range(C)]

            def graph_whole(hi, lo, g):
                return [(hi[:, g, c, :], lo[:, g, c, :]) for c in range(C)]

            def turn_matrix(i, src):
                bank = prep_bank(i)
                for k in range(C):
                    for c in range(C):
                        last = pe.transpose(bank[:, k, c * P:(c + 1) * P], src[:, c, k * P:(k + 1) * P], ident[:])
                last.then_inc(s_prep, 1)

            pe.wait_ge(s_consts, 4)
            pe.wait_ge(s_load["adj"], 16)
            turn_matrix(0, adj_nat)
            pe.wait_ge(s_load["u3"], 16)
            turn_matrix(1, u3_nat)
            pe.wait_ge(s_halves, 1)
            turn_matrix(2, w4_nat)
            pe.wait_ge(s_halves, 2)
            turn_matrix(3, w3_nat)
            pe.wait_ge(s_halves, 3)
            pe.wait_ge(s_prep_lo, 1)
            turn_matrix(4, w5_nat)
            pe.wait_ge(s_load["u5"], 16)
            pe.wait_ge(s_prep_lo, 2)
            turn_matrix(5, u5_nat)

            def prepare_back():
                pe.wait_ge(s_load["v"], 16)
                pe.wait_ge(s_prep_lo, 3)
                turn_matrix(6, wv_nat)
                pe.wait_ge(s_load["qk"], 32)
                pe.wait_ge(s_prep_lo, 4)
                bank = prep_bank(7)
                for k in range(C):
                    for c in range(C):
                        last = pe.matmul(bank[:, k, :], wq_nat[:, c, k * P:(k + 1) * P], wk_nat[:, c, :],
                                         start=c == 0, stop=c == C - 1)
                last.then_inc(s_prep, 1)
                pe.wait_ge(s_rows, 1)
                pe.wait_ge(s_prep_lo, 5)
                turn_matrix(8, adj_rows)

            def turn_input(p):
                pe.wait_ge(s_x_front, 16 * p + 16)
                if later(p):
                    pe.wait_ge(front.s_z, 4 * p)
                for k in range(C):
                    for g in range(G):
                        for c in range(C):
                            last = pe.transpose(front.ps0[:, k, g * N + c * P:g * N + (c + 1) * P],
                                                x_front[:, g, c, k * P:(k + 1) * P], ident[:])
                    last.then_inc(s_in_turned, 1)

            def mix(L, n, turned=0):
                S = L.state
                pe.wait_ge(S.s_node_lo, upto(n))
                if L is back and later(n):
                    pe.wait_ge(s_ax_lo, 4 * n)
                if L is front and later(n):
                    pe.wait_ge(L.s_tanh, 2 * n)
                if later(turned):
                    pe.wait_ge(state_b.s_node_lo, turned)
                for k in range(C):
                    for g in range(G):
                        last = product(L.ps1[:, k, g * N:(g + 1) * N],
                                       graph_columns(S.node_hi, S.node_lo, g, k), whole(adjT))
                    last.then_inc(L.s_mixed, 1)

            def base(L, n):
                S = L.state
                pe.wait_ge(S.s_feat_lo, upto(n))
                if L is back and later(n):
                    pe.wait_ge(s_sum, 8 * n)
                for k in range(C):
                    product(L.ps0[:, k], columns(u3T, k), [(S.feat_hi[:, c], S.feat_lo[:, c]) for c in range(C)],
                            ).then_inc(L.s_base, 1)

            def mixed(L):
                return [(L.a_hi[:, c], L.a_lo[:, c]) for c in range(C)]

            def reset(L, n):
                pe.wait_ge(L.s_a_lo, upto(n))
                for k in range(C):
                    product(L.ps1[:, k], columns(w4T, k), mixed(L)).then_inc(L.s_reset, 1)

            def update(L, n):
                for k in range(C):
                    pe.wait_ge(L.s_base_kept, upto(n, k))
                    product(L.ps0[:, k], columns(w3T, k), mixed(L), start=False).then_inc(L.s_update, 1)

            def candidate_mixed(L, n):
                for k in range(C):
                    pe.wait_ge(L.s_reset_arg, upto(n, k))
                    product(L.ps1[:, k], columns(w5T, k), mixed(L), stop=False)

            def candidate_reset(L, n):
                pe.wait_ge(L.s_rh_lo, upto(n))
                for k in range(C):
                    product(L.ps1[:, k], columns(u5T, k), [(L.rh_hi[:, c], L.rh_lo[:, c]) for c in range(C)],
                            start=False).then_inc(L.s_cand, 1)

            def turn(L, n, source, ready, count, done):
                pe.wait_ge(ready, count)
                for g in range(G):
                    for c in range(C):
                        for k in range(C):
                            last = pe.transpose(L.ps1[:, g, c * D + k * P:c * D + (k + 1) * P],
                                                source[:, k, g * N + c * P:g * N + (c + 1) * P], ident[:])
                    last.then_inc(done, 1)

            def turn_x1(q, g):
                pe.wait_ge(s_normed, ln(q, 0, g))
                for k in range(C):
                    for c in range(C):
                        last = pe.transpose(back.ps1[:, g, k * N + c * P:k * N + (c + 1) * P],
                                            normed[:, g, c, k * P:(k + 1) * P], ident[:])
                last.then_inc(s_x1_turned, 1)

            def keys(q, g):
                pe.wait_ge(s_x1_lo, upto(q, g))
                for k in range(C):
                    last = product(back.ps0[:, g, k * N:(k + 1) * N], columns(wqk, k), graph_whole(x_hi, x_lo, g))
                last.then_inc(s_y, 1)

            def values(q, g):
                for c in range(C):
                    last = product(back.ps1[:, g, c * D:(c + 1) * D], graph_columns(x_hi, x_lo, g, c), whole(wvT))
                last.then_inc(s_v, 1)

            def relate(q, g):
                pe.wait_ge(s_y_lo, upto(q, g))
                for c in range(C):
                    last = product(back.ps0[:, g, c * N:(c + 1) * N], graph_columns(x_hi, x_lo, g, c),
                                   graph_whole(y_hi, y_lo, g))
                last.then_inc(s_rel, 1)

            def sum_squares(q, g):
                pe.wait_ge(s_v_lo, upto(q, g))
                pe.wait_ge(s_rel_sq, upto(q, g))
                for c in range(C):
                    for m in range(C):
                        last = pe.matmul(back.ps1[:, g, c:c + 1], rel_sq[:, g, m, c * P:(c + 1) * P], ones[:],
                                         start=m == 0, stop=m == C - 1, skip_group_check=True)
                last.then_inc(s_norm, 1)

            def attend(q, g):
                pe.wait_ge(s_rel_lo, upto(q, g))
                for c in range(C):
                    last = product(back.ps0[:, g, c * D:(c + 1) * D], graph_columns(rel_hi, rel_lo, g, c),
                                   graph_whole(v_hi, v_lo, g))
                last.then_inc(s_attended, 1)

            def mix_nodes(q, j, g):
                pe.wait_ge(s_x_lo, conv(q, j, g))
                if j == 0:
                    pe.wait_ge(s_norm_sq, q + 1)
                for k in range(C):
                    last = product(back.ps1[:, g, k * N:(k + 1) * N], graph_columns(x_hi, x_lo, g, k),
                                   whole((adjT, norm_adjT)[j]))
                last.then_inc(s_ax, 1)

            def convolve(q, j, g):
                pe.wait_ge(s_ax_lo, conv(q, j, g))
                for c in range(C):
                    last = product(back.ps0[:, g, c * D:(c + 1) * D], graph_columns(y_hi, y_lo, g, c),
                                   whole((w2s, w3s)[j]))
                last.then_inc(s_conv, 1)

            def body(p, q):
                if p is not None:
                    turn_input(p)
                if q is not None:
                    mix(back, q)
                    base(back, q)
                    reset(back, q)
                if p is not None:
                    base(front, 2 * p)
                    mix(front, 2 * p, 2 * p)
                if q is not None:
                    update(back, q)
                    candidate_mixed(back, q)
                if p is not None:
                    reset(front, 2 * p)
                if q is not None:
                    candidate_reset(back, q)
                if p is not None:
                    update(front, 2 * p)
                    candidate_mixed(front, 2 * p)
                if q is not None:
                    turn(back, q, h3, s_h3, upto(q), s_h3_turned)
                if p is not None:
                    candidate_reset(front, 2 * p)
                if q is not None:
                    for g in range(G):
                        turn_x1(q, g)
                    for g in range(G):
                        keys(q, g)
                if p is not None:
                    turn(front, 2 * p, state_f.feat, state_f.s_feat, upto(2 * p + 1), state_f.s_turned)
                if q is not None:
                    for g in range(G):
                        values(q, g)
                if p is not None:
                    base(front, 2 * p + 1)
                if q is not None:
                    for g in range(G):
                        relate(q, g)
                if p is not None:
                    mix(front, 2 * p + 1, 2 * p)
                if q is not None:
                    for g in range(G):
                        sum_squares(q, g)
                    for g in range(G):
                        attend(q, g)
                if p is not None:
                    reset(front, 2 * p + 1)
                    update(front, 2 * p + 1)
                if q is not None:
                    for g in range(G):
                        mix_nodes(q, 0, g)
                if p is not None:
                    candidate_mixed(front, 2 * p + 1)
                if q is not None:
                    for g in range(G):
                        convolve(q, 0, g)
                if p is not None:
                    candidate_reset(front, 2 * p + 1)
                if q is not None:
                    for g in range(G):
                        mix_nodes(q, 1, g)
                if p is not None:
                    turn(front, 2 * p + 1, state_b.feat, state_b.s_feat, upto(p), state_b.s_turned)
                if q is not None:
                    for g in range(G):
                        convolve(q, 1, g)

            pe.wait_ge(s_prep_lo, 6)
            prepare_back()
            body(0, None)
            pe.wait_ge(s_prep_lo, len(prepared) + 2)
            body(1, 0)
            with pe.Fori(2, PAIRS) as p:
                body(p, p - 1)
            body(None, LAST)

        @block.scalar
        def _(act):
            def copy(dst, src):
                return act.activation(dst, src, ACT.Copy)

            for i in range(8):
                act.wait_ge(s_prep, i + 1)
                copy(prepared[i].hi[:], prep_bank(i)).then_inc(s_prep_hi, 1)
            act.wait_ge(s_norm_full, 1)
            copy(norm_adjT.hi[:], norm_full).then_inc(s_prep_hi, 1)
            act.wait_ge(s_load["l23"], 32)
            copy(w2s.hi[:], w2_nat).then_inc(s_prep_hi, 1)
            copy(w3s.hi[:], w3s_nat).then_inc(s_prep_hi, 1)
            act.wait_ge(s_bias, 3)

            def input_hi(p):
                S = state_f
                act.wait_ge(s_x_front, 16 * p + 16)
                if later(p):
                    act.wait_ge(front.s_mixed, 4 * p)
                for g in range(G):
                    copy(S.node_hi[:, g], x_front[:, g]).then_inc(S.s_node_hi, 1)
                if later(p):
                    act.wait_ge(front.s_base, 4 * p)
                    act.wait_ge(front.s_kept, 4 * p)
                    act.wait_ge(front.s_rh, 4 * p)
                for k in range(C):
                    act.wait_ge(s_in_turned, upto(p, k))
                    copy(S.feat_hi[:, k], front.ps0[:, k]).then_inc(S.s_feat_hi, 1)
                    copy(S.feat[:, k], front.ps0[:, k]).then_inc(S.s_feat, 1)

            def a_hi(L, n):
                for k in range(C):
                    act.wait_ge(L.s_mixed, upto(n, k))
                    copy(L.a_hi[:, k], L.ps1[:, k]).then_inc(L.s_a_hi, 1)

            def keep_base(L, n):
                for k in range(C):
                    act.wait_ge(L.s_base, upto(n, k))
                    act.activation(L.gate[:, k], L.ps0[:, k], ACT.Identity,
                                   bias=bias_r[:, k:k + 1]).then_inc(L.s_base_kept, 1)

            def reset_gate(L, n):
                for k in range(C):
                    act.wait_ge(L.s_reset_arg, upto(n, k))
                    act.activation(L.gate[:, k], L.gate[:, k], ACT.Sigmoid).then_inc(L.s_r, 1)

            def rh_hi(L, n):
                for k in range(C):
                    act.wait_ge(L.s_rh, upto(n, k))
                    copy(L.rh_hi[:, k], L.gate[:, k]).then_inc(L.s_rh_hi, 1)

            def update_gate(L, n):
                for k in range(C):
                    act.wait_ge(L.s_update, upto(n, k))
                    act.activation(L.z[:, k], L.ps0[:, k], ACT.Sigmoid, bias=bias_z[:, k:k + 1]).then_inc(L.s_z, 1)

            def candidate(L, n):
                for k in range(C):
                    act.wait_ge(L.s_cand, upto(n, k))
                    act.activation(L.cand[:, k], L.ps1[:, k], ACT.Tanh, bias=bias_c[:, k:k + 1]).then_inc(L.s_tanh, 1)

            def feat_hi(S, v):
                for k in range(C):
                    act.wait_ge(S.s_feat, upto(v, k))
                    copy(S.feat_hi[:, k], S.feat[:, k]).then_inc(S.s_feat_hi, 1)

            def node_hi(S, v, turned):
                for g in range(G):
                    act.wait_ge(S.s_turned, turned + g + 1)
                    copy(S.node_hi[:, g], front.ps1[:, g].rearrange("p (c d) -> p c d", c=C)).then_inc(S.s_node_hi, 1)

            def graph_hi(dst, src, ready, count, g, done):
                act.wait_ge(ready, count)
                copy(dst[:, g].rearrange("p c n -> p (c n)"), src).then_inc(done, 1)

            def x1_hi(q, g):
                graph_hi(x_hi, back.ps1[:, g], s_x1_turned, upto(q, g), g, s_x1_hi)

            def keys_hi(q, g):
                graph_hi(y_hi, back.ps0[:, g], s_y, upto(q, g), g, s_y_hi)

            def values_hi(q, g):
                graph_hi(v_hi, back.ps1[:, g], s_v, upto(q, g), g, s_v_hi)

            def relation_hi(q, g):
                act.wait_ge(s_masked, upto(q, g))
                act.activation(rel_sq[:, g], rel[:, g], ACT.Square).then_inc(s_rel_sq, 1)
                copy(rel_hi[:, g], rel[:, g]).then_inc(s_rel_hi, 1)

            def conv_x_hi(q, j, g):
                act.wait_ge(s_normed, ln(q, j + 1, g))
                copy(x_hi[:, g], normed[:, g]).then_inc(s_x_hi, 1)

            def conv_ax_hi(q, j, g):
                graph_hi(y_hi, back.ps1[:, g], s_ax, conv(q, j, g), g, s_ax_hi)

            def body(p, q):
                if p is not None:
                    input_hi(p)
                if q is not None:
                    a_hi(back, q)
                    keep_base(back, q)
                    reset_gate(back, q)
                    rh_hi(back, q)
                if p is not None:
                    keep_base(front, 2 * p)
                    a_hi(front, 2 * p)
                if q is not None:
                    update_gate(back, q)
                if p is not None:
                    reset_gate(front, 2 * p)
                    rh_hi(front, 2 * p)
                if q is not None:
                    candidate(back, q)
                if p is not None:
                    update_gate(front, 2 * p)
                    candidate(front, 2 * p)
                    feat_hi(state_f, 2 * p + 1)
                if q is not None:
                    for g in range(G):
                        x1_hi(q, g)
                    for g in range(G):
                        keys_hi(q, g)
                if p is not None:
                    node_hi(state_f, 2 * p + 1, 2 * p)
                if q is not None:
                    for g in range(G):
                        values_hi(q, g)
                if p is not None:
                    keep_base(front, 2 * p + 1)
                if q is not None:
                    for g in range(G):
                        relation_hi(q, g)
                if p is not None:
                    a_hi(front, 2 * p + 1)
                    reset_gate(front, 2 * p + 1)
                    rh_hi(front, 2 * p + 1)
                    update_gate(front, 2 * p + 1)
                if q is not None:
                    for g in range(G):
                        conv_x_hi(q, 0, g)
                    for g in range(G):
                        conv_ax_hi(q, 0, g)
                if p is not None:
                    candidate(front, 2 * p + 1)
                    feat_hi(state_b, p)
                if q is not None:
                    for g in range(G):
                        conv_x_hi(q, 1, g)
                if p is not None:
                    node_hi(state_b, p, 2 * p)
                if q is not None:
                    for g in range(G):
                        conv_ax_hi(q, 1, g)

            body(0, None)
            body(1, 0)
            with act.Fori(2, PAIRS) as p:
                body(p, p - 1)
            body(None, LAST)

        @block.vector
        def _(dve):
            def full(t):
                return t.bitcast(F32)

            def prep_lo(i, src):
                dve.wait_ge(s_prep_hi, i + 1)
                m = (prepared + [w2s, w3s])[i]
                dve.tensor_tensor(m.lo[:], src, full(m.hi[:]), ALU.subtract).then_inc(s_prep_lo, 1)

            prep_lo(0, prep_bank(0))
            for w, name in ((w4_nat, "w4"), (w3_nat, "w3"), (w5_nat, "w5")):
                dve.wait_ge(s_load[name], 16)
                dve.tensor_tensor(w[:, :, 0:D], w[:, :, 0:D], w[:, :, D:2 * D], ALU.add).then_inc(s_halves, 1)
            for i in range(1, 6):
                prep_lo(i, prep_bank(i))
            dve.wait_ge(s_load["bias"], 16 * 7)
            dve.tensor_tensor(bias_z[:], bias_in[:, 0], bias_in[:, 1], ALU.add).then_inc(s_bias, 1)
            dve.tensor_tensor(bias_r[:], bias_in[:, 2], bias_in[:, 1], ALU.add).then_inc(s_bias, 1)
            dve.tensor_tensor(bias_c[:], bias_in[:, 3], bias_in[:, 4], ALU.add).then_inc(s_bias, 1)
            dve.wait_ge(s_load["adj"], 16)
            dve.tensor_reduce(deg[:], adj_nat[:], AX.X, ALU.add).then_inc(s_deg, 1)
            dve.wait_ge(s_deg, 1)
            dve.tensor_scalar(deg_floor[:], deg[:], TINY, None, ALU.max).then_inc(s_deg, 1)
            dve.tensor_scalar(deg_pos[:], deg[:], 0.0, None, ALU.is_gt).then_inc(s_deg, 1)
            dve.wait_ge(s_deg, 3)
            dve.wait_ge(s_deg_pow, 1)
            dve.tensor_tensor(deg_inv[:], deg_pow[:], deg_pos[:], ALU.mult).then_inc(s_deg, 1)
            dve.wait_ge(s_deg, 4)
            for c in range(C):
                last = dve.tensor_scalar(adj_rows[:, c], adj_nat[:, c], deg_inv[:, c:c + 1], None, ALU.mult)
            last.then_inc(s_rows, 1)
            prep_lo(6, prep_bank(6))
            prep_lo(7, prep_bank(7))
            dve.wait_ge(s_prep, 9)
            for c in range(C):
                last = dve.tensor_scalar(norm_full[:, c], prep_bank(8)[:, c], deg_inv[:, c:c + 1], None, ALU.mult)
            last.then_inc(s_norm_full, 1)
            prep_lo(8, norm_full)
            prep_lo(9, w2_nat)
            prep_lo(10, w3s_nat)

            def input_lo(p):
                S = state_f
                for g in range(G):
                    dve.wait_ge(S.s_node_hi, upto(2 * p, g))
                    dve.tensor_tensor(S.node_lo[:, g], x_front[:, g], full(S.node_hi[:, g]),
                                      ALU.subtract).then_inc(S.s_node_lo, 1)
                for k in range(C):
                    dve.wait_ge(S.s_feat, upto(2 * p, k))
                    dve.tensor_tensor(S.feat_lo[:, k], front.ps0[:, k], full(S.feat_hi[:, k]),
                                      ALU.subtract).then_inc(S.s_feat_lo, 1)

            def a_lo(L, n):
                for k in range(C):
                    dve.wait_ge(L.s_a_hi, upto(n, k))
                    dve.tensor_tensor(L.a_lo[:, k], L.ps1[:, k], full(L.a_hi[:, k]),
                                      ALU.subtract).then_inc(L.s_a_lo, 1)

            def reset_arg(L, n):
                for k in range(C):
                    dve.wait_ge(L.s_base_kept, upto(n, k))
                    dve.wait_ge(L.s_reset, upto(n, k))
                    dve.tensor_tensor(L.gate[:, k], L.ps1[:, k], L.gate[:, k], ALU.add).then_inc(L.s_reset_arg, 1)

            def reset_h(L, n):
                S = L.state
                dve.wait_ge(S.s_feat, upto(n))
                for k in range(C):
                    dve.wait_ge(L.s_r, upto(n, k))
                    dve.tensor_tensor(L.gate[:, k], L.gate[:, k], S.feat[:, k], ALU.mult).then_inc(L.s_rh, 1)
                for k in range(C):
                    dve.wait_ge(L.s_rh_hi, upto(n, k))
                    dve.tensor_tensor(L.rh_lo[:, k], L.gate[:, k], full(L.rh_hi[:, k]),
                                      ALU.subtract).then_inc(L.s_rh_lo, 1)

            def new_h(L, n, dst, done):
                for k in range(C):
                    dve.wait_ge(L.s_tanh, upto(n, k))
                    dve.tensor_tensor(L.cand[:, k], L.z[:, k], L.cand[:, k], ALU.mult).then_inc(L.s_zc, 1)
                for k in range(C):
                    dve.wait_ge(L.s_kept, upto(n, k))
                    dve.wait_ge(L.s_zc, upto(n, k))
                    dve.tensor_tensor(dst[:, k], L.kept[:, k], L.cand[:, k], ALU.add).then_inc(done, 1)

            def feat_lo(S, v):
                for k in range(C):
                    dve.wait_ge(S.s_feat_hi, upto(v, k))
                    dve.tensor_tensor(S.feat_lo[:, k], S.feat[:, k], full(S.feat_hi[:, k]),
                                      ALU.subtract).then_inc(S.s_feat_lo, 1)

            def node_lo(S, v):
                for g in range(G):
                    dve.wait_ge(S.s_node_hi, upto(v, g))
                    dve.tensor_tensor(S.node_lo[:, g], front.ps1[:, g].rearrange("p (c d) -> p c d", c=C),
                                      full(S.node_hi[:, g]), ALU.subtract).then_inc(S.s_node_lo, 1)

            def moments_of(q, j, g):
                dve.wait_ge(s_sum, ln(q, j, g))
                for c in range(C):
                    last = dve.bn_stats(stats[:, g, c], summed[:, g, c])
                last.then_inc(s_stats, 1)
                dve.wait_ge(s_stats, ln(q, j, g))
                dve.memset(pad[:], 0.0)
                for c in range(C):
                    last = dve.bn_aggr(moments[:, g, c], stats[:, g, c])
                last.then_inc(s_moments, 1)
                dve.wait_ge(s_moments, ln(q, j, g))
                dve.tensor_scalar(var_eps[:, g], moments[:, g, :, 1], EPS, None, ALU.add).then_inc(s_var, 1)

            def normalise(q, j, g, dst):
                dve.wait_ge(s_rstd, ln(q, j, g))
                for c in range(C):
                    last = dve.tensor_scalar(dst[:, g, c], summed[:, g, c], moments[:, g, c, 0:1],
                                             rstd[:, g, c:c + 1], ALU.subtract, ALU.mult)
                last.then_inc(s_normed, 1)

            def graph_bank(ps, g):
                return ps[:, g].rearrange("p (c d) -> p c d", c=C)

            def sum_gnn(q, g):
                dve.wait_ge(s_x_back, 16 * q + 16)
                dve.wait_ge(s_h3_turned, upto(q, g))
                dve.tensor_tensor(summed[:, g], graph_bank(back.ps1, g), x_back[:, g], ALU.add).then_inc(s_sum, 1)

            def sum_attended(q, g):
                dve.wait_ge(s_norm_inv, q + 1)
                dve.wait_ge(s_attended, upto(q, g))
                for c in range(C):
                    last = dve.scalar_tensor_tensor(summed[:, g, c], back.ps0[:, g, c * D:(c + 1) * D],
                                                    norm_inv[:, g, c:c + 1], normed[:, g, c], ALU.mult, ALU.add)
                last.then_inc(s_sum, 1)

            def sum_conv(q, j, g):
                dve.wait_ge(s_skip, conv(q, j, g))
                dve.wait_ge(s_conv, conv(q, j, g))
                dve.tensor_tensor(summed[:, g], graph_bank(back.ps0, g), skip[:, g], ALU.add).then_inc(s_sum, 1)

            def graph_lo(lo, hi, src, ready, count, g, done):
                dve.wait_ge(ready, count)
                dve.tensor_tensor(lo[:, g], src, full(hi[:, g]), ALU.subtract).then_inc(done, 1)

            def x1_lo(q, g):
                graph_lo(x_lo, x_hi, graph_bank(back.ps1, g), s_x1_hi, upto(q, g), g, s_x1_lo)

            def keys_lo(q, g):
                graph_lo(y_lo, y_hi, graph_bank(back.ps0, g), s_y_hi, upto(q, g), g, s_y_lo)

            def values_lo(q, g):
                graph_lo(v_lo, v_hi, graph_bank(back.ps1, g), s_v_hi, upto(q, g), g, s_v_lo)

            def mask(q, g):
                dve.wait_ge(s_rel, upto(q, g))
                dve.tensor_tensor(rel[:, g], graph_bank(back.ps0, g), adj_nat[:], ALU.mult).then_inc(s_masked, 1)

            def relation_lo(q, g):
                graph_lo(rel_lo, rel_hi, rel[:, g], s_rel_hi, upto(q, g), g, s_rel_lo)

            def norms(q):
                dve.wait_ge(s_norm, upto(q))
                dve.tensor_copy(norm_sq[:], back.ps1[:, :, 0:C]).then_inc(s_norm_sq, 1)

            def conv_x_lo(q, j, g):
                graph_lo(x_lo, x_hi, normed[:, g], s_x_hi, conv(q, j, g), g, s_x_lo)

            def conv_ax_lo(q, j, g):
                graph_lo(y_lo, y_hi, graph_bank(back.ps1, g), s_ax_hi, conv(q, j, g), g, s_ax_lo)

            def body(p, q):
                if p is not None:
                    input_lo(p)
                if q is not None:
                    a_lo(back, q)
                    reset_arg(back, q)
                    reset_h(back, q)
                if p is not None:
                    a_lo(front, 2 * p)
                    reset_arg(front, 2 * p)
                    reset_h(front, 2 * p)
                if q is not None:
                    new_h(back, q, h3, s_h3)
                    for g in range(G):
                        sum_gnn(q, g)
                        moments_of(q, 0, g)
                    for g in range(G):
                        normalise(q, 0, g, normed)
                if p is not None:
                    new_h(front, 2 * p, state_f.feat, state_f.s_feat)
                if q is not None:
                    for g in range(G):
                        x1_lo(q, g)
                if p is not None:
                    feat_lo(state_f, 2 * p + 1)
                if q is not None:
                    for g in range(G):
                        keys_lo(q, g)
                if p is not None:
                    node_lo(state_f, 2 * p + 1)
                if q is not None:
                    for g in range(G):
                        values_lo(q, g)
                    for g in range(G):
                        mask(q, g)
                    for g in range(G):
                        relation_lo(q, g)
                if p is not None:
                    a_lo(front, 2 * p + 1)
                if q is not None:
                    norms(q)
                    for g in range(G):
                        sum_attended(q, g)
                        moments_of(q, 1, g)
                    for g in range(G):
                        normalise(q, 1, g, normed)
                if p is not None:
                    reset_arg(front, 2 * p + 1)
                    reset_h(front, 2 * p + 1)
                if q is not None:
                    for g in range(G):
                        conv_x_lo(q, 0, g)
                    for g in range(G):
                        conv_ax_lo(q, 0, g)
                    for g in range(G):
                        sum_conv(q, 0, g)
                        moments_of(q, 2, g)
                    for g in range(G):
                        normalise(q, 2, g, normed)
                if p is not None:
                    new_h(front, 2 * p + 1, state_b.feat, state_b.s_feat)
                    feat_lo(state_b, p)
                if q is not None:
                    for g in range(G):
                        conv_x_lo(q, 1, g)
                if p is not None:
                    node_lo(state_b, p)
                if q is not None:
                    for g in range(G):
                        conv_ax_lo(q, 1, g)
                    if later(q):
                        dve.wait_ge(s_stored, 16 * q)
                    for g in range(G):
                        sum_conv(q, 1, g)
                        moments_of(q, 3, g)
                    for g in range(G):
                        normalise(q, 3, g, result)

            body(0, None)
            body(1, 0)
            with dve.Fori(2, PAIRS) as p:
                body(p, p - 1)
            body(None, LAST)


_INS = ["x", "adj", "L0_gnn_w3_w", "L0_gnn_w3_b", "L0_gnn_u3_w", "L0_gnn_u3_b", "L0_gnn_w4_w", "L0_gnn_w4_b",
        "L0_gnn_w5_w", "L0_gnn_w5_b", "L0_gnn_u5_w", "L0_gnn_u5_b", "L1_gnn_Wq", "L1_gnn_Wk", "L1_gnn_Wv",
        "L2_gnn_weight", "L2_gnn_bias", "L3_gnn_weight", "L3_gnn_bias"]


def kernel(**inputs):
    import numpy as _np
    import concourse.bacc as _bacc
    from concourse.bass_utils import run_bass_kernel_spmd as _run

    nc = _bacc.Bacc("TRN2", target_bir_lowering=False, num_devices=1)
    arrays, args = {}, []
    for name in _INS:
        a = _np.ascontiguousarray(inputs[name])
        arrays[f"in_{name}"] = a
        args.append(nc.dram_tensor(f"in_{name}", a.shape, mybir.dt.from_np(a.dtype), kind="ExternalInput").ap())
    shape = inputs["x"].shape
    args.append(nc.dram_tensor("out_0", shape, F32, kind="ExternalOutput").ap())
    build(nc, *args)
    r = _run(nc, [arrays], core_ids=[0])
    return r.results[0]["out_0"]
```

```python
from contextlib import ExitStack

import concourse.bass as bass
from concourse import mybir

P = 128
F32 = mybir.dt.float32
F32R = mybir.dt.float32r
ALU = mybir.AluOpType
ACT = mybir.ActivationFunctionType
AX = mybir.AxisListType
EPS = 1e-5
TINY = 1.1754944e-38


class Split:

    def __init__(self, hi, lo):
        self.hi, self.lo = hi, lo


class State:

    def __init__(self, sb, sem, name, full, by_graph):
        self.feat = sb(f"{name}_feat", full)
        self.feat_hi, self.feat_lo = sb(f"{name}_feat_hi", full, F32R), sb(f"{name}_feat_lo", full, F32R)
        self.node_hi, self.node_lo = sb(f"{name}_node_hi", by_graph, F32R), sb(f"{name}_node_lo", by_graph, F32R)
        self.s_feat = sem(f"{name}_s_feat")
        self.s_feat_hi, self.s_feat_lo = sem(f"{name}_s_feat_hi"), sem(f"{name}_s_feat_lo")
        self.s_turned = sem(f"{name}_s_turned")
        self.s_node_hi, self.s_node_lo = sem(f"{name}_s_node_hi"), sem(f"{name}_s_node_lo")


class Lane:

    def __init__(self, sb, psum, sem, name, state, full):
        self.state = state
        self.ps0, self.ps1 = psum(f"{name}_ps0", full), psum(f"{name}_ps1", full)
        self.a_hi, self.a_lo = sb(f"{name}_a_hi", full, F32R), sb(f"{name}_a_lo", full, F32R)
        self.gate = sb(f"{name}_gate", full)
        self.rh_hi, self.rh_lo = sb(f"{name}_rh_hi", full, F32R), sb(f"{name}_rh_lo", full, F32R)
        self.z = sb(f"{name}_z", full)
        self.kept = sb(f"{name}_kept", full)
        self.cand = sb(f"{name}_cand", full)
        self.s_mixed = sem("{}_s_mixed".format(name))
        self.s_a_hi = sem("{}_s_a_hi".format(name))
        self.s_a_lo = sem("{}_s_a_lo".format(name))
        self.s_base = sem("{}_s_base".format(name))
        self.s_base_kept = sem("{}_s_base_kept".format(name))
        self.s_reset = sem("{}_s_reset".format(name))
        self.s_reset_arg = sem("{}_s_reset_arg".format(name))
        self.s_r = sem("{}_s_r".format(name))
        self.s_rh = sem("{}_s_rh".format(name))
        self.s_rh_hi = sem("{}_s_rh_hi".format(name))
        self.s_rh_lo = sem("{}_s_rh_lo".format(name))
        self.s_update = sem("{}_s_update".format(name))
        self.s_z = sem("{}_s_z".format(name))
        self.s_zh = sem("{}_s_zh".format(name))
        self.s_kept = sem("{}_s_kept".format(name))
        self.s_cand = sem("{}_s_cand".format(name))
        self.s_tanh = sem("{}_s_tanh".format(name))
        self.s_zc = sem("{}_s_zc".format(name))


def build(nc, x, adj, w3_w, w3_b, u3_w, u3_b, w4_w, w4_b, w5_w, w5_b, u5_w, u5_b, wq, wk, wv,
          l2_w, l2_b, l3_w, l3_b, out):
    B, N, D = x.shape
    C = N // P
    G = 2
    T = G * N
    PAIRS = B // G
    assert N == D and C == 2 and T == 512
    LAST = PAIRS - 1

    x_pairs = x.rearrange("(q g) (c p) d -> q p g c d", g=G, p=P)
    out_pairs = out.rearrange("(q g) (c p) d -> q p g c d", g=G, p=P)

    with ExitStack() as ctx:
        def sb(name, shape, dt=F32):
            return ctx.enter_context(nc.sbuf_tensor(name, shape, dt))

        def sem(name):
            return ctx.enter_context(nc.semaphore(name))

        def split_matrix(name):
            return Split(sb(name + "_hi", [P, C, D], F32R), sb(name + "_lo", [P, C, D], F32R))

        adjT = split_matrix("adjT")
        norm_adjT = split_matrix("norm_adjT")
        w3T = split_matrix("w3T")
        w4T = split_matrix("w4T")
        w5T = split_matrix("w5T")
        u3T = split_matrix("u3T")
        u5T = split_matrix("u5T")
        wvT = split_matrix("wvT")
        wqk = split_matrix("wqk")
        w2s = split_matrix("w2s")
        w3s = split_matrix("w3s")

        ident = sb("ident", [P, P])
        adj_nat = sb("adj_nat", [P, C, N])
        ones = sb("ones", [P, 1])
        neg_half = sb("neg_half", [P, C])
        bias_in = sb("bias_in", [P, 5, C])
        bias_z = sb("bias_z", [P, C])
        bias_r = sb("bias_r", [P, C])
        bias_c = sb("bias_c", [P, C])
        bias_out = sb("bias_out", [P, 2, C, D])
        deg = sb("deg", [P, C])
        deg_floor = sb("deg_floor", [P, C])
        deg_pos = sb("deg_pos", [P, C])
        deg_pow = sb("deg_pow", [P, C])
        deg_inv = sb("deg_inv", [P, C])

        def psum(name, shape):
            return ctx.enter_context(nc.psum_tensor(name, shape, F32))

        state_f = State(sb, sem, "hf", [P, C, T], [P, G, C, D])
        state_b = State(sb, sem, "hb", [P, C, T], [P, G, C, D])
        front = Lane(sb, psum, sem, "f", state_f, [P, C, T])
        back = Lane(sb, psum, sem, "b", state_b, [P, C, T])

        def per_graph(t):
            return t[:].rearrange("p c (k n) -> p c k n", k=C)

        x_front = sb("x_front", [P, G, C, D])
        x_back = sb("x_back", [P, G, C, D])
        h3 = back.cand
        summed = sb("summed", [P, G, C, D])
        normed = sb("normed", [P, G, C, D])
        skip = sb("skip", [P, G, C, D])
        result = sb("result", [P, G, C, D])
        x_hi, x_lo = per_graph(back.a_hi), per_graph(back.a_lo)
        y_hi, y_lo = per_graph(back.rh_hi), per_graph(back.rh_lo)
        v_hi, v_lo = sb("v_hi", [P, G, C, D], F32R), sb("v_lo", [P, G, C, D], F32R)
        rel, rel_sq = per_graph(back.gate), per_graph(back.z)
        rel_hi, rel_lo = sb("rel_hi", [P, G, C, N], F32R), sb("rel_lo", [P, G, C, N], F32R)
        stats = sb("stats", [P, G, C, 6])
        moments = sb("moments", [P, G, C, 2])
        pad = sb("pad", [P, 1])
        var_eps = sb("var_eps", [P, G, C])
        rstd = sb("rstd", [P, G, C])
        norm_sq = sb("norm_sq", [P, G, C])
        norm_inv = sb("norm_inv", [P, G, C])

        w3_nat, w4_nat, w5_nat = back.gate[:], back.z[:], back.kept[:]
        flat = lambda t: t[:].rearrange("p g c d -> p (g c) d")
        u3_nat, u5_nat = flat(x_back)[:, 0:C], flat(x_back)[:, C:2 * C]
        wq_nat, wk_nat = flat(summed)[:, 0:C], flat(summed)[:, C:2 * C]
        wv_nat, w2_nat = flat(normed)[:, 0:C], flat(normed)[:, C:2 * C]
        w3s_nat = flat(skip)[:, 0:C]
        adj_rows, norm_full = flat(result)[:, 0:C], flat(result)[:, C:2 * C]

        s_x_front, s_x_back, s_stored = sem("s_x_front"), sem("s_x_back"), sem("s_stored")
        s_load = {n: sem("s_load_" + n) for n in ("adj", "u3", "w4", "w3", "w5", "u5", "qk", "v", "l23", "bias")}
        s_consts, s_bias, s_halves = sem("s_consts"), sem("s_bias"), sem("s_halves")
        s_deg, s_deg_pow, s_rows, s_norm_full = sem("s_deg"), sem("s_deg_pow"), sem("s_rows"), sem("s_norm_full")
        s_prep, s_prep_hi, s_prep_lo = sem("s_prep"), sem("s_prep_hi"), sem("s_prep_lo")
        s_in_turned = sem("s_in_turned")
        s_h3, s_h3_turned = sem("s_h3"), sem("s_h3_turned")
        s_sum, s_stats, s_moments, s_var, s_rstd, s_normed = (
            sem("s_sum"), sem("s_stats"), sem("s_moments"), sem("s_var"), sem("s_rstd"), sem("s_normed"))
        s_x1_turned, s_x1_hi, s_x1_lo = sem("s_x1_turned"), sem("s_x1_hi"), sem("s_x1_lo")
        s_y, s_y_hi, s_y_lo = sem("s_y"), sem("s_y_hi"), sem("s_y_lo")
        s_v, s_v_hi, s_v_lo = sem("s_v"), sem("s_v_hi"), sem("s_v_lo")
        s_rel, s_masked, s_rel_hi, s_rel_sq, s_rel_lo = (
            sem("s_rel"), sem("s_masked"), sem("s_rel_hi"), sem("s_rel_sq"), sem("s_rel_lo"))
        s_norm, s_norm_sq, s_norm_inv, s_attended = sem("s_norm"), sem("s_norm_sq"), sem("s_norm_inv"), sem("s_attended")
        s_x_hi, s_x_lo, s_skip = sem("s_x_hi"), sem("s_x_lo"), sem("s_skip")
        s_ax, s_ax_hi, s_ax_lo, s_conv = sem("s_ax"), sem("s_ax_hi"), sem("s_ax_lo"), sem("s_conv")

        def upto(n, k=1):
            return 2 * n + k + 1

        def ln(q, j, g):
            return 8 * q + 2 * j + g + 1

        def conv(q, j, g=1):
            return 4 * q + 2 * j + g + 1

        prepared = [adjT, u3T, w4T, w3T, w5T, u5T, wvT, wqk, norm_adjT]

        def prep_bank(i):
            ps = (back.ps0, back.ps1)[i // 2 % 2]
            return ps[:, i % 2, :].rearrange("p (c n) -> p c n", c=C)

        def later(n):
            return not (isinstance(n, int) and n == 0)

        block = ctx.enter_context(nc.Block())

        @block.sync
        def _(sp):
            def rows(w):
                return w.rearrange("(c p) d -> p c d", p=P)

            sp.dma_start(adj_nat[:], rows(adj)).then_inc(s_load["adj"], 16)
            sp.dma_start(x_front[:], x_pairs[0]).then_inc(s_x_front, 16)
            sp.dma_start(u3_nat, rows(u3_w)).then_inc(s_load["u3"], 16)
            sp.dma_start(w4_nat, rows(w4_w)).then_inc(s_load["w4"], 16)
            sp.dma_start(w3_nat, rows(w3_w)).then_inc(s_load["w3"], 16)
            sp.dma_start(w5_nat, rows(w5_w)).then_inc(s_load["w5"], 16)
            sp.dma_start(u5_nat, rows(u5_w)).then_inc(s_load["u5"], 16)
            sp.dma_start(wv_nat, rows(wv)).then_inc(s_load["v"], 16)
            sp.dma_start(wq_nat, rows(wq)).then_inc(s_load["qk"], 16)
            sp.dma_start(wk_nat, rows(wk)).then_inc(s_load["qk"], 16)
            sp.dma_start(w2_nat, rows(l2_w)).then_inc(s_load["l23"], 16)
            sp.dma_start(w3s_nat, rows(l3_w)).then_inc(s_load["l23"], 16)

            def load_front(p):
                sp.wait_ge(s_in_turned, upto(p - 1))
                sp.wait_ge(state_f.s_node_lo, upto(2 * p - 2))
                sp.dma_start(x_front[:], x_pairs[p]).then_inc(s_x_front, 16)

            def load_back(q):
                sp.wait_ge(s_sum, ln(q - 1, 0, 1))
                sp.dma_start(x_back[:], x_pairs[q]).then_inc(s_x_back, 16)

            def store(q):
                sp.wait_ge(s_normed, ln(q, 3, 1))
                sp.dma_start(out_pairs[q], result[:]).then_inc(s_stored, 16)

            load_front(1)
            sp.wait_ge(s_prep, 6)
            sp.dma_start(x_back[:], x_pairs[0]).then_inc(s_x_back, 16)
            with sp.Fori(1, LAST) as p:
                load_front(p + 1)
                load_back(p)
                store(p - 1)
            load_back(LAST)
            store(LAST - 1)
            store(LAST)
            sp.wait_ge(s_stored, 16 * PAIRS)

        @block.gpsimd
        def _(pool):
            pool.memset(ident[:], 0.0).then_inc(s_consts, 1)
            pool.memset(ones[:], 1.0).then_inc(s_consts, 1)
            pool.memset(neg_half[:], -0.5).then_inc(s_consts, 1)
            pool.wait_ge(s_consts, 3)
            pool.affine_select(out=ident[:], in_=ident[:], compare_op=ALU.not_equal, fill=1.0, base=0,
                               pattern=[[-1, P]], channel_multiplier=1).then_inc(s_consts, 1)
            for i, b in enumerate((w3_b, u3_b, w4_b, w5_b, u5_b)):
                pool.dma_start(bias_in[:, i, :], b.rearrange("(c p) -> p c", p=P),
                               allow_slow_non_contiguous=True).then_inc(s_load["bias"], 16)
            for i, b in enumerate((l2_b, l3_b)):
                for c in range(C):
                    pool.dma_start(bias_out[:, i, c, :], b.partition_broadcast(P)).then_inc(s_load["bias"], 16)

            pool.wait_ge(s_deg, 3)
            pool.tensor_tensor(deg_pow[:], deg_floor[:], neg_half[:], ALU.pow).then_inc(s_deg_pow, 1)

            def update_h(L, n, k):
                pool.wait_ge(L.state.s_feat, upto(n, k))
                pool.wait_ge(L.s_z, upto(n, k))
                pool.tensor_tensor(L.kept[:, k], L.z[:, k], L.state.feat[:, k], ALU.mult).then_inc(L.s_zh, 1)

            def keep(L, n, k):
                pool.wait_ge(L.s_zh, upto(n, k))
                pool.tensor_tensor(L.kept[:, k], L.state.feat[:, k], L.kept[:, k], ALU.subtract).then_inc(L.s_kept, 1)

            def inverse_std(q, j, g):
                pool.wait_ge(s_var, ln(q, j, g))
                pool.tensor_tensor(rstd[:, g], var_eps[:, g], neg_half[:], ALU.pow).then_inc(s_rstd, 1)

            def inverse_norm(q, g):
                pool.wait_ge(s_norm_sq, upto(q, g))
                pool.tensor_tensor(norm_inv[:, g], norm_sq[:, g], neg_half[:], ALU.pow).then_inc(s_norm_inv, 1)

            def add_bias(q, j, g):
                pool.wait_ge(s_normed, ln(q, j + 1, g))
                pool.tensor_tensor(skip[:, g], normed[:, g], bias_out[:, j], ALU.add).then_inc(s_skip, 1)

            def body(p, q):
                if q is not None:
                    for k in range(2):
                        update_h(back, q, k)
                    for k in range(2):
                        keep(back, q, k)
                    inverse_std(q, 0, 0)
                if p is not None:
                    update_h(front, 2 * p, 0)
                if q is not None:
                    inverse_std(q, 0, 1)
                if p is not None:
                    keep(front, 2 * p, 0)
                    update_h(front, 2 * p, 1)
                    keep(front, 2 * p, 1)
                if q is not None:
                    inverse_norm(q, 0)
                    inverse_std(q, 1, 0)
                    inverse_norm(q, 1)
                    add_bias(q, 0, 0)
                    inverse_std(q, 1, 1)
                    add_bias(q, 0, 1)
                    inverse_std(q, 2, 0)
                if p is not None:
                    update_h(front, 2 * p + 1, 0)
                    keep(front, 2 * p + 1, 0)
                if q is not None:
                    inverse_std(q, 2, 1)
                if p is not None:
                    update_h(front, 2 * p + 1, 1)
                    keep(front, 2 * p + 1, 1)
                if q is not None:
                    for k in range(2):
                        add_bias(q, 1, k)
                    for k in range(2):
                        inverse_std(q, 3, k)

            pool.wait_ge(s_load["bias"], 16 * 9)
            body(0, None)
            body(1, 0)
            with pool.Fori(2, PAIRS) as p:
                body(p, p - 1)
            body(None, LAST)

        @block.tensor
        def _(pe):
            def product(bank, stationary, moving, start=True, stop=True):
                terms = [(s, m) for (sh, sl), (mh, ml) in zip(stationary, moving)
                         for s, m in ((sh, mh), (sh, ml), (sl, mh))]
                for i, (s, m) in enumerate(terms):
                    last = pe.matmul(bank, s, m, start=start and i == 0, stop=stop and i == len(terms) - 1,
                                     skip_group_check=True)
                return last

            def columns(m, k):
                return [(m.hi[:, c, k * P:(k + 1) * P], m.lo[:, c, k * P:(k + 1) * P]) for c in range(C)]

            def whole(m):
                return [(m.hi[:, c, :], m.lo[:, c, :]) for c in range(C)]

            def graph_columns(hi, lo, g, k):
                return [(hi[:, g, c, k * P:(k + 1) * P], lo[:, g, c, k * P:(k + 1) * P]) for c in range(C)]

            def graph_whole(hi, lo, g):
                return [(hi[:, g, c, :], lo[:, g, c, :]) for c in range(C)]

            def turn_matrix(i, src):
                bank = prep_bank(i)
                for k in range(C):
                    for c in range(C):
                        last = pe.transpose(bank[:, k, c * P:(c + 1) * P], src[:, c, k * P:(k + 1) * P], ident[:])
                last.then_inc(s_prep, 1)

            pe.wait_ge(s_consts, 4)
            pe.wait_ge(s_load["adj"], 16)
            turn_matrix(0, adj_nat)
            pe.wait_ge(s_load["u3"], 16)
            turn_matrix(1, u3_nat)
            pe.wait_ge(s_halves, 1)
            turn_matrix(2, w4_nat)
            pe.wait_ge(s_halves, 2)
            turn_matrix(3, w3_nat)
            pe.wait_ge(s_halves, 3)
            pe.wait_ge(s_prep_lo, 1)
            turn_matrix(4, w5_nat)
            pe.wait_ge(s_load["u5"], 16)
            pe.wait_ge(s_prep_lo, 2)
            turn_matrix(5, u5_nat)

            def prepare_back():
                pe.wait_ge(s_load["v"], 16)
                pe.wait_ge(s_prep_lo, 3)
                turn_matrix(6, wv_nat)
                pe.wait_ge(s_load["qk"], 32)
                pe.wait_ge(s_prep_lo, 4)
                bank = prep_bank(7)
                for k in range(C):
                    for c in range(C):
                        last = pe.matmul(bank[:, k, :], wq_nat[:, c, k * P:(k + 1) * P], wk_nat[:, c, :],
                                         start=c == 0, stop=c == C - 1)
                last.then_inc(s_prep, 1)
                pe.wait_ge(s_rows, 1)
                pe.wait_ge(s_prep_lo, 5)
                turn_matrix(8, adj_rows)

            def turn_input(p, k):
                pe.wait_ge(s_x_front, 16 * p + 16)
                if later(p):
                    pe.wait_ge(front.s_z, upto(2 * p - 1, k))
                for g in range(G):
                    for c in range(C):
                        last = pe.transpose(front.ps0[:, k, g * N + c * P:g * N + (c + 1) * P],
                                            x_front[:, g, c, k * P:(k + 1) * P], ident[:])
                last.then_inc(s_in_turned, 1)

            def mix(L, n, k, pair=None):
                S = L.state
                pe.wait_ge(S.s_node_lo, upto(n))
                if L is back and later(n):
                    pe.wait_ge(s_ax_lo, conv(n - 1, 1, k))
                if pair is not None and later(pair):
                    pe.wait_ge(state_b.s_node_lo, upto(pair - 1, k))
                for g in range(G):
                    last = product(L.ps1[:, k, g * N:(g + 1) * N],
                                   graph_columns(S.node_hi, S.node_lo, g, k), whole(adjT))
                last.then_inc(L.s_mixed, 1)

            def base(L, n, k):
                S = L.state
                pe.wait_ge(S.s_feat_lo, upto(n))
                if L is back and later(n):
                    pe.wait_ge(s_sum, ln(n - 1, 3, k))
                product(L.ps0[:, k], columns(u3T, k),
                        [(S.feat_hi[:, c], S.feat_lo[:, c]) for c in range(C)]).then_inc(L.s_base, 1)

            def mixed(L):
                return [(L.a_hi[:, c], L.a_lo[:, c]) for c in range(C)]

            def reset(L, n, k):
                pe.wait_ge(L.s_a_lo, upto(n))
                product(L.ps1[:, k], columns(w4T, k), mixed(L)).then_inc(L.s_reset, 1)

            def update(L, n, k):
                pe.wait_ge(L.s_a_lo, upto(n))
                pe.wait_ge(L.s_base_kept, upto(n, k))
                product(L.ps0[:, k], columns(w3T, k), mixed(L), start=False).then_inc(L.s_update, 1)

            def candidate_mixed(L, n, k):
                pe.wait_ge(L.s_reset_arg, upto(n, k))
                product(L.ps1[:, k], columns(w5T, k), mixed(L), stop=False)

            def candidate_reset(L, n, k):
                pe.wait_ge(L.s_rh_lo, upto(n))
                product(L.ps1[:, k], columns(u5T, k), [(L.rh_hi[:, c], L.rh_lo[:, c]) for c in range(C)],
                        start=False).then_inc(L.s_cand, 1)

            def turn(ps1, g, feat, done):
                for c in range(C):
                    for k in range(C):
                        last = pe.transpose(ps1[:, g, c * D + k * P:c * D + (k + 1) * P],
                                            feat[:, k, g * N + c * P:g * N + (c + 1) * P], ident[:])
                last.then_inc(done, 1)

            def turn_h(S, v, g):
                pe.wait_ge(S.s_feat, upto(v))
                turn(front.ps1, g, S.feat, S.s_turned)

            def turn_h3(q, g):
                pe.wait_ge(s_h3, upto(q))
                turn(back.ps1, g, h3, s_h3_turned)

            def turn_x1(q, g):
                pe.wait_ge(s_normed, ln(q, 0, g))
                for k in range(C):
                    for c in range(C):
                        last = pe.transpose(back.ps1[:, g, k * N + c * P:k * N + (c + 1) * P],
                                            normed[:, g, c, k * P:(k + 1) * P], ident[:])
                last.then_inc(s_x1_turned, 1)

            def keys(q, g):
                pe.wait_ge(s_x1_lo, upto(q, g))
                for k in range(C):
                    last = product(back.ps0[:, g, k * N:(k + 1) * N], columns(wqk, k), graph_whole(x_hi, x_lo, g))
                last.then_inc(s_y, 1)

            def values(q, g):
                pe.wait_ge(s_x1_lo, upto(q, g))
                for c in range(C):
                    last = product(back.ps1[:, g, c * D:(c + 1) * D], graph_columns(x_hi, x_lo, g, c), whole(wvT))
                last.then_inc(s_v, 1)

            def relate(q, g):
                pe.wait_ge(s_y_lo, upto(q, g))
                for c in range(C):
                    last = product(back.ps0[:, g, c * N:(c + 1) * N], graph_columns(x_hi, x_lo, g, c),
                                   graph_whole(y_hi, y_lo, g))
                last.then_inc(s_rel, 1)

            def sum_squares(q, g):
                pe.wait_ge(s_v_lo, upto(q, g))
                pe.wait_ge(s_rel_sq, upto(q, g))
                for c in range(C):
                    for m in range(C):
                        last = pe.matmul(back.ps1[:, g, c:c + 1], rel_sq[:, g, m, c * P:(c + 1) * P], ones[:],
                                         start=m == 0, stop=m == C - 1, skip_group_check=True)
                last.then_inc(s_norm, 1)

            def attend(q, g):
                pe.wait_ge(s_v_lo, upto(q, g))
                pe.wait_ge(s_rel_lo, upto(q, g))
                for c in range(C):
                    last = product(back.ps0[:, g, c * D:(c + 1) * D], graph_columns(rel_hi, rel_lo, g, c),
                                   graph_whole(v_hi, v_lo, g))
                last.then_inc(s_attended, 1)

            def mix_nodes(q, j, g):
                pe.wait_ge(s_x_lo, conv(q, j, g))
                if j == 0:
                    pe.wait_ge(s_norm_sq, upto(q, g))
                for k in range(C):
                    last = product(back.ps1[:, g, k * N:(k + 1) * N], graph_columns(x_hi, x_lo, g, k),
                                   whole((adjT, norm_adjT)[j]))
                last.then_inc(s_ax, 1)

            def convolve(q, j, g):
                pe.wait_ge(s_ax_lo, conv(q, j, g))
                for c in range(C):
                    last = product(back.ps0[:, g, c * D:(c + 1) * D], graph_columns(y_hi, y_lo, g, c),
                                   whole((w2s, w3s)[j]))
                last.then_inc(s_conv, 1)

            def body(p, q):
                if p is not None:
                    turn_input(p, 0)
                if q is not None:
                    base(back, q, 0)
                    for k in range(2):
                        mix(back, q, k)
                if p is not None:
                    turn_input(p, 1)
                if q is not None:
                    base(back, q, 1)
                    for k in range(2):
                        reset(back, q, k)
                    for k in range(2):
                        update(back, q, k)
                    candidate_mixed(back, q, 0)
                if p is not None:
                    mix(front, 2 * p, 0, p)
                if q is not None:
                    candidate_mixed(back, q, 1)
                if p is not None:
                    mix(front, 2 * p, 1, p)
                if q is not None:
                    for k in range(2):
                        candidate_reset(back, q, k)
                if p is not None:
                    for k in range(2):
                        base(front, 2 * p, k)
                if q is not None:
                    for k in range(2):
                        turn_h3(q, k)
                if p is not None:
                    for k in range(2):
                        reset(front, 2 * p, k)
                    update(front, 2 * p, 0)
                    candidate_mixed(front, 2 * p, 0)
                    update(front, 2 * p, 1)
                if q is not None:
                    turn_x1(q, 0)
                if p is not None:
                    candidate_reset(front, 2 * p, 0)
                    candidate_mixed(front, 2 * p, 1)
                if q is not None:
                    keys(q, 0)
                    turn_x1(q, 1)
                if p is not None:
                    candidate_reset(front, 2 * p, 1)
                if q is not None:
                    values(q, 0)
                    relate(q, 0)
                    keys(q, 1)
                if p is not None:
                    turn_h(state_f, 2 * p + 1, 0)
                if q is not None:
                    values(q, 1)
                if p is not None:
                    turn_h(state_f, 2 * p + 1, 1)
                if q is not None:
                    sum_squares(q, 0)
                    attend(q, 0)
                    relate(q, 1)
                if p is not None:
                    base(front, 2 * p + 1, 0)
                    mix(front, 2 * p + 1, 0)
                if q is not None:
                    sum_squares(q, 1)
                if p is not None:
                    mix(front, 2 * p + 1, 1)
                if q is not None:
                    attend(q, 1)
                    mix_nodes(q, 0, 0)
                if p is not None:
                    base(front, 2 * p + 1, 1)
                    for k in range(2):
                        reset(front, 2 * p + 1, k)
                if q is not None:
                    convolve(q, 0, 0)
                    mix_nodes(q, 0, 1)
                if p is not None:
                    update(front, 2 * p + 1, 0)
                    candidate_mixed(front, 2 * p + 1, 0)
                if q is not None:
                    convolve(q, 0, 1)
                if p is not None:
                    update(front, 2 * p + 1, 1)
                    candidate_reset(front, 2 * p + 1, 0)
                    candidate_mixed(front, 2 * p + 1, 1)
                    candidate_reset(front, 2 * p + 1, 1)
                if q is not None:
                    for k in range(2):
                        mix_nodes(q, 1, k)
                if p is not None:
                    turn_h(state_b, p, 0)
                if q is not None:
                    convolve(q, 1, 0)
                if p is not None:
                    turn_h(state_b, p, 1)
                if q is not None:
                    convolve(q, 1, 1)

            pe.wait_ge(s_prep_lo, 6)
            prepare_back()
            body(0, None)
            pe.wait_ge(s_prep_lo, len(prepared) + 2)
            body(1, 0)
            with pe.Fori(2, PAIRS) as p:
                body(p, p - 1)
            body(None, LAST)

        @block.scalar
        def _(act):
            def copy(dst, src):
                return act.activation(dst, src, ACT.Copy)

            for i in range(8):
                act.wait_ge(s_prep, i + 1)
                copy(prepared[i].hi[:], prep_bank(i)).then_inc(s_prep_hi, 1)
            act.wait_ge(s_norm_full, 1)
            copy(norm_adjT.hi[:], norm_full).then_inc(s_prep_hi, 1)
            act.wait_ge(s_load["l23"], 32)
            copy(w2s.hi[:], w2_nat).then_inc(s_prep_hi, 1)
            copy(w3s.hi[:], w3s_nat).then_inc(s_prep_hi, 1)
            act.wait_ge(s_bias, 3)

            def input_nodes_hi(p, g):
                act.wait_ge(s_x_front, 16 * p + 16)
                if later(p):
                    act.wait_ge(front.s_mixed, upto(2 * p - 1))
                copy(state_f.node_hi[:, g], x_front[:, g]).then_inc(state_f.s_node_hi, 1)

            def input_hi(p, k):
                if later(p):
                    act.wait_ge(front.s_base, upto(2 * p - 1))
                    act.wait_ge(front.s_kept, upto(2 * p - 1))
                    act.wait_ge(front.s_rh, upto(2 * p - 1))
                act.wait_ge(s_in_turned, upto(p, k))
                copy(state_f.feat_hi[:, k], front.ps0[:, k]).then_inc(state_f.s_feat_hi, 1)
                copy(state_f.feat[:, k], front.ps0[:, k]).then_inc(state_f.s_feat, 1)

            def a_hi(L, n, k):
                act.wait_ge(L.s_mixed, upto(n, k))
                copy(L.a_hi[:, k], L.ps1[:, k]).then_inc(L.s_a_hi, 1)

            def keep_base(L, n, k):
                act.wait_ge(L.s_base, upto(n, k))
                act.activation(L.gate[:, k], L.ps0[:, k], ACT.Identity, bias=bias_r[:, k:k + 1]).then_inc(L.s_base_kept, 1)

            def reset_gate(L, n, k):
                act.wait_ge(L.s_reset_arg, upto(n, k))
                act.activation(L.gate[:, k], L.gate[:, k], ACT.Sigmoid).then_inc(L.s_r, 1)

            def rh_hi(L, n, k):
                act.wait_ge(L.s_rh, upto(n, k))
                copy(L.rh_hi[:, k], L.gate[:, k]).then_inc(L.s_rh_hi, 1)

            def update_gate(L, n, k):
                act.wait_ge(L.s_update, upto(n, k))
                act.activation(L.z[:, k], L.ps0[:, k], ACT.Sigmoid, bias=bias_z[:, k:k + 1]).then_inc(L.s_z, 1)

            def candidate(L, n, k):
                act.wait_ge(L.s_cand, upto(n, k))
                act.activation(L.cand[:, k], L.ps1[:, k], ACT.Tanh, bias=bias_c[:, k:k + 1]).then_inc(L.s_tanh, 1)

            def feat_hi(S, v, k):
                act.wait_ge(S.s_feat, upto(v, k))
                if S is state_b and later(v):
                    act.wait_ge(back.s_base, upto(v - 1))
                copy(S.feat_hi[:, k], S.feat[:, k]).then_inc(S.s_feat_hi, 1)

            def node_hi(S, v, g, turned):
                act.wait_ge(S.s_turned, turned)
                if S is state_b and later(v):
                    act.wait_ge(back.s_mixed, upto(v - 1))
                copy(S.node_hi[:, g].rearrange("p c d -> p (c d)"), front.ps1[:, g]).then_inc(S.s_node_hi, 1)

            def graph_hi(dst, src, ready, count, g, done):
                act.wait_ge(ready, count)
                copy(dst[:, g].rearrange("p c n -> p (c n)"), src).then_inc(done, 1)

            def x1_hi(q, g):
                graph_hi(x_hi, back.ps1[:, g], s_x1_turned, upto(q, g), g, s_x1_hi)

            def keys_hi(q, g):
                graph_hi(y_hi, back.ps0[:, g], s_y, upto(q, g), g, s_y_hi)

            def values_hi(q, g):
                graph_hi(v_hi, back.ps1[:, g], s_v, upto(q, g), g, s_v_hi)

            def relation_hi(q, g):
                act.wait_ge(s_masked, upto(q, g))
                copy(rel_hi[:, g], rel[:, g]).then_inc(s_rel_hi, 1)

            def relation_squares(q, g):
                act.wait_ge(s_masked, upto(q, g))
                act.activation(rel_sq[:, g], rel[:, g], ACT.Square).then_inc(s_rel_sq, 1)

            def conv_x_hi(q, j, g):
                act.wait_ge(s_normed, ln(q, j + 1, g))
                copy(x_hi[:, g], normed[:, g]).then_inc(s_x_hi, 1)

            def conv_ax_hi(q, j, g):
                graph_hi(y_hi, back.ps1[:, g], s_ax, conv(q, j, g), g, s_ax_hi)

            def body(p, q):
                if q is not None:
                    a_hi(back, q, 0)
                if p is not None:
                    input_nodes_hi(p, 0)
                if q is not None:
                    a_hi(back, q, 1)
                if p is not None:
                    input_nodes_hi(p, 1)
                if q is not None:
                    keep_base(back, q, 0)
                if p is not None:
                    for k in range(2):
                        input_hi(p, k)
                if q is not None:
                    keep_base(back, q, 1)
                    reset_gate(back, q, 0)
                    rh_hi(back, q, 0)
                    update_gate(back, q, 0)
                    reset_gate(back, q, 1)
                    rh_hi(back, q, 1)
                if p is not None:
                    a_hi(front, 2 * p, 0)
                if q is not None:
                    update_gate(back, q, 1)
                if p is not None:
                    a_hi(front, 2 * p, 1)
                if q is not None:
                    for k in range(2):
                        candidate(back, q, k)
                if p is not None:
                    for k in range(2):
                        keep_base(front, 2 * p, k)
                    for k in range(2):
                        reset_gate(front, 2 * p, k)
                    for k in range(2):
                        rh_hi(front, 2 * p, k)
                    for k in range(2):
                        update_gate(front, 2 * p, k)
                if q is not None:
                    x1_hi(q, 0)
                if p is not None:
                    candidate(front, 2 * p, 0)
                if q is not None:
                    keys_hi(q, 0)
                    x1_hi(q, 1)
                if p is not None:
                    candidate(front, 2 * p, 1)
                    for k in range(2):
                        feat_hi(state_f, 2 * p + 1, k)
                if q is not None:
                    values_hi(q, 0)
                    relation_squares(q, 0)
                    keys_hi(q, 1)
                    relation_hi(q, 0)
                if p is not None:
                    for k in range(2):
                        node_hi(state_f, 2 * p + 1, k, 2 * p + k + 1)
                if q is not None:
                    values_hi(q, 1)
                    relation_hi(q, 1)
                    relation_squares(q, 1)
                if p is not None:
                    a_hi(front, 2 * p + 1, 0)
                    keep_base(front, 2 * p + 1, 0)
                if q is not None:
                    conv_x_hi(q, 0, 0)
                if p is not None:
                    a_hi(front, 2 * p + 1, 1)
                if q is not None:
                    conv_ax_hi(q, 0, 0)
                if p is not None:
                    keep_base(front, 2 * p + 1, 1)
                if q is not None:
                    conv_x_hi(q, 0, 1)
                if p is not None:
                    for k in range(2):
                        reset_gate(front, 2 * p + 1, k)
                    rh_hi(front, 2 * p + 1, 0)
                if q is not None:
                    conv_ax_hi(q, 0, 1)
                if p is not None:
                    rh_hi(front, 2 * p + 1, 1)
                    for k in range(2):
                        update_gate(front, 2 * p + 1, k)
                if q is not None:
                    conv_x_hi(q, 1, 0)
                if p is not None:
                    candidate(front, 2 * p + 1, 0)
                if q is not None:
                    conv_x_hi(q, 1, 1)
                if p is not None:
                    candidate(front, 2 * p + 1, 1)
                    feat_hi(state_b, p, 0)
                if q is not None:
                    for k in range(2):
                        conv_ax_hi(q, 1, k)
                if p is not None:
                    feat_hi(state_b, p, 1)
                    for k in range(2):
                        node_hi(state_b, p, k, 2 * p + k + 1)

            body(0, None)
            body(1, 0)
            with act.Fori(2, PAIRS) as p:
                body(p, p - 1)
            body(None, LAST)

        @block.vector
        def _(dve):
            def full(t):
                return t.bitcast(F32)

            def prep_lo(i, src):
                dve.wait_ge(s_prep_hi, i + 1)
                m = (prepared + [w2s, w3s])[i]
                dve.tensor_tensor(m.lo[:], src, full(m.hi[:]), ALU.subtract).then_inc(s_prep_lo, 1)

            prep_lo(0, prep_bank(0))
            for w, name in ((w4_nat, "w4"), (w3_nat, "w3"), (w5_nat, "w5")):
                dve.wait_ge(s_load[name], 16)
                dve.tensor_tensor(w[:, :, 0:D], w[:, :, 0:D], w[:, :, D:2 * D], ALU.add).then_inc(s_halves, 1)
            for i in range(1, 6):
                prep_lo(i, prep_bank(i))
            dve.wait_ge(s_load["bias"], 16 * 9)
            dve.tensor_tensor(bias_z[:], bias_in[:, 0], bias_in[:, 1], ALU.add).then_inc(s_bias, 1)
            dve.tensor_tensor(bias_r[:], bias_in[:, 2], bias_in[:, 1], ALU.add).then_inc(s_bias, 1)
            dve.tensor_tensor(bias_c[:], bias_in[:, 3], bias_in[:, 4], ALU.add).then_inc(s_bias, 1)
            dve.wait_ge(s_load["adj"], 16)
            dve.tensor_reduce(deg[:], adj_nat[:], AX.X, ALU.add).then_inc(s_deg, 1)
            dve.wait_ge(s_deg, 1)
            dve.tensor_scalar(deg_floor[:], deg[:], TINY, None, ALU.max).then_inc(s_deg, 1)
            dve.tensor_scalar(deg_pos[:], deg[:], 0.0, None, ALU.is_gt).then_inc(s_deg, 1)
            dve.wait_ge(s_deg, 3)
            dve.wait_ge(s_deg_pow, 1)
            dve.tensor_tensor(deg_inv[:], deg_pow[:], deg_pos[:], ALU.mult).then_inc(s_deg, 1)
            dve.wait_ge(s_deg, 4)
            for c in range(C):
                last = dve.tensor_scalar(adj_rows[:, c], adj_nat[:, c], deg_inv[:, c:c + 1], None, ALU.mult)
            last.then_inc(s_rows, 1)
            prep_lo(6, prep_bank(6))
            prep_lo(7, prep_bank(7))
            dve.wait_ge(s_prep, 9)
            for c in range(C):
                last = dve.tensor_scalar(norm_full[:, c], prep_bank(8)[:, c], deg_inv[:, c:c + 1], None, ALU.mult)
            last.then_inc(s_norm_full, 1)
            prep_lo(8, norm_full)
            prep_lo(9, w2_nat)
            prep_lo(10, w3s_nat)

            def input_nodes_lo(p, g):
                S = state_f
                dve.wait_ge(S.s_node_hi, upto(2 * p, g))
                dve.tensor_tensor(S.node_lo[:, g], x_front[:, g], full(S.node_hi[:, g]),
                                  ALU.subtract).then_inc(S.s_node_lo, 1)

            def input_lo(p, k):
                S = state_f
                dve.wait_ge(S.s_feat, upto(2 * p, k))
                dve.tensor_tensor(S.feat_lo[:, k], front.ps0[:, k], full(S.feat_hi[:, k]),
                                  ALU.subtract).then_inc(S.s_feat_lo, 1)

            def a_lo(L, n, k):
                dve.wait_ge(L.s_a_hi, upto(n, k))
                dve.tensor_tensor(L.a_lo[:, k], L.ps1[:, k], full(L.a_hi[:, k]), ALU.subtract).then_inc(L.s_a_lo, 1)

            def reset_arg(L, n, k):
                dve.wait_ge(L.s_base_kept, upto(n, k))
                dve.wait_ge(L.s_reset, upto(n, k))
                dve.tensor_tensor(L.gate[:, k], L.ps1[:, k], L.gate[:, k], ALU.add).then_inc(L.s_reset_arg, 1)

            def reset_h(L, n, k):
                dve.wait_ge(L.state.s_feat, upto(n, k))
                dve.wait_ge(L.s_r, upto(n, k))
                dve.tensor_tensor(L.gate[:, k], L.gate[:, k], L.state.feat[:, k], ALU.mult).then_inc(L.s_rh, 1)

            def rh_lo(L, n, k):
                dve.wait_ge(L.s_rh_hi, upto(n, k))
                dve.tensor_tensor(L.rh_lo[:, k], L.gate[:, k], full(L.rh_hi[:, k]), ALU.subtract).then_inc(L.s_rh_lo, 1)

            def candidate_part(L, n, k):
                dve.wait_ge(L.s_tanh, upto(n, k))
                dve.tensor_tensor(L.cand[:, k], L.z[:, k], L.cand[:, k], ALU.mult).then_inc(L.s_zc, 1)

            def new_h(L, n, k, dst, done):
                dve.wait_ge(L.s_kept, upto(n, k))
                dve.wait_ge(L.s_zc, upto(n, k))
                dve.tensor_tensor(dst[:, k], L.kept[:, k], L.cand[:, k], ALU.add).then_inc(done, 1)

            def hand_over_h(p, k):
                if later(p):
                    dve.wait_ge(back.s_kept, upto(p - 1, k))
                new_h(front, 2 * p + 1, k, state_b.feat, state_b.s_feat)

            def feat_lo(S, v, k):
                dve.wait_ge(S.s_feat_hi, upto(v, k))
                dve.tensor_tensor(S.feat_lo[:, k], S.feat[:, k], full(S.feat_hi[:, k]),
                                  ALU.subtract).then_inc(S.s_feat_lo, 1)

            def node_lo(S, v, g):
                dve.wait_ge(S.s_node_hi, upto(v, g))
                dve.tensor_tensor(S.node_lo[:, g], front.ps1[:, g].rearrange("p (c d) -> p c d", c=C),
                                  full(S.node_hi[:, g]), ALU.subtract).then_inc(S.s_node_lo, 1)

            def moments_of(q, j, g):
                dve.wait_ge(s_sum, ln(q, j, g))
                for c in range(C):
                    last = dve.bn_stats(stats[:, g, c], summed[:, g, c])
                last.then_inc(s_stats, 1)
                dve.wait_ge(s_stats, ln(q, j, g))
                dve.memset(pad[:], 0.0)
                for c in range(C):
                    last = dve.bn_aggr(moments[:, g, c], stats[:, g, c])
                last.then_inc(s_moments, 1)
                dve.wait_ge(s_moments, ln(q, j, g))
                dve.tensor_scalar(var_eps[:, g], moments[:, g, :, 1], EPS, None, ALU.add).then_inc(s_var, 1)

            def normalise(q, j, g, dst):
                dve.wait_ge(s_rstd, ln(q, j, g))
                if j == 2:
                    dve.wait_ge(s_skip, conv(q, 0, g))
                if j == 3 and later(q):
                    dve.wait_ge(s_stored, 16 * q)
                for c in range(C):
                    last = dve.tensor_scalar(dst[:, g, c], summed[:, g, c], moments[:, g, c, 0:1],
                                             rstd[:, g, c:c + 1], ALU.subtract, ALU.mult)
                last.then_inc(s_normed, 1)

            def graph_bank(ps, g):
                return ps[:, g].rearrange("p (c d) -> p c d", c=C)

            def sum_gnn(q, g):
                dve.wait_ge(s_x_back, 16 * q + 16)
                dve.wait_ge(s_h3_turned, upto(q, g))
                dve.tensor_tensor(summed[:, g], graph_bank(back.ps1, g), x_back[:, g], ALU.add).then_inc(s_sum, 1)

            def sum_attended(q, g):
                dve.wait_ge(s_norm_inv, upto(q, g))
                dve.wait_ge(s_attended, upto(q, g))
                for c in range(C):
                    last = dve.scalar_tensor_tensor(summed[:, g, c], back.ps0[:, g, c * D:(c + 1) * D],
                                                    norm_inv[:, g, c:c + 1], normed[:, g, c], ALU.mult, ALU.add)
                last.then_inc(s_sum, 1)

            def sum_conv(q, j, g):
                dve.wait_ge(s_skip, conv(q, j, g))
                dve.wait_ge(s_conv, conv(q, j, g))
                dve.tensor_tensor(summed[:, g], graph_bank(back.ps0, g), skip[:, g], ALU.add).then_inc(s_sum, 1)

            def graph_lo(lo, hi, src, ready, count, g, done):
                dve.wait_ge(ready, count)
                dve.tensor_tensor(lo[:, g], src, full(hi[:, g]), ALU.subtract).then_inc(done, 1)

            def x1_lo(q, g):
                graph_lo(x_lo, x_hi, graph_bank(back.ps1, g), s_x1_hi, upto(q, g), g, s_x1_lo)

            def keys_lo(q, g):
                graph_lo(y_lo, y_hi, graph_bank(back.ps0, g), s_y_hi, upto(q, g), g, s_y_lo)

            def values_lo(q, g):
                graph_lo(v_lo, v_hi, graph_bank(back.ps1, g), s_v_hi, upto(q, g), g, s_v_lo)

            def mask(q, g):
                dve.wait_ge(s_rel, upto(q, g))
                dve.tensor_tensor(rel[:, g], graph_bank(back.ps0, g), adj_nat[:], ALU.mult).then_inc(s_masked, 1)

            def relation_lo(q, g):
                graph_lo(rel_lo, rel_hi, rel[:, g], s_rel_hi, upto(q, g), g, s_rel_lo)

            def norms(q, g):
                dve.wait_ge(s_norm, upto(q, g))
                dve.tensor_copy(norm_sq[:, g], back.ps1[:, g, 0:C]).then_inc(s_norm_sq, 1)

            def conv_x_lo(q, j, g):
                graph_lo(x_lo, x_hi, normed[:, g], s_x_hi, conv(q, j, g), g, s_x_lo)

            def conv_ax_lo(q, j, g):
                graph_lo(y_lo, y_hi, graph_bank(back.ps1, g), s_ax_hi, conv(q, j, g), g, s_ax_lo)

            def body(p, q):
                if q is not None:
                    for k in range(2):
                        a_lo(back, q, k)
                if p is not None:
                    input_nodes_lo(p, 0)
                if q is not None:
                    reset_arg(back, q, 0)
                if p is not None:
                    input_nodes_lo(p, 1)
                if q is not None:
                    reset_h(back, q, 0)
                    reset_arg(back, q, 1)
                    rh_lo(back, q, 0)
                    reset_h(back, q, 1)
                    rh_lo(back, q, 1)
                if p is not None:
                    for k in range(2):
                        input_lo(p, k)
                    for k in range(2):
                        a_lo(front, 2 * p, k)
                if q is not None:
                    candidate_part(back, q, 0)
                    new_h(back, q, 0, h3, s_h3)
                    candidate_part(back, q, 1)
                    new_h(back, q, 1, h3, s_h3)
                    sum_gnn(q, 0)
                    moments_of(q, 0, 0)
                if p is not None:
                    reset_arg(front, 2 * p, 0)
                if q is not None:
                    sum_gnn(q, 1)
                if p is not None:
                    reset_arg(front, 2 * p, 1)
                    for k in range(2):
                        reset_h(front, 2 * p, k)
                    rh_lo(front, 2 * p, 0)
                if q is not None:
                    normalise(q, 0, 0, normed)
                if p is not None:
                    rh_lo(front, 2 * p, 1)
                if q is not None:
                    moments_of(q, 0, 1)
                    x1_lo(q, 0)
                    normalise(q, 0, 1, normed)
                if p is not None:
                    candidate_part(front, 2 * p, 0)
                if q is not None:
                    keys_lo(q, 0)
                if p is not None:
                    new_h(front, 2 * p, 0, state_f.feat, state_f.s_feat)
                if q is not None:
                    x1_lo(q, 1)
                if p is not None:
                    candidate_part(front, 2 * p, 1)
                    new_h(front, 2 * p, 1, state_f.feat, state_f.s_feat)
                if q is not None:
                    mask(q, 0)
                if p is not None:
                    feat_lo(state_f, 2 * p + 1, 0)
                if q is not None:
                    values_lo(q, 0)
                    relation_lo(q, 0)
                if p is not None:
                    feat_lo(state_f, 2 * p + 1, 1)
                if q is not None:
                    keys_lo(q, 1)
                    norms(q, 0)
                if p is not None:
                    node_lo(state_f, 2 * p + 1, 0)
                if q is not None:
                    values_lo(q, 1)
                    sum_attended(q, 0)
                if p is not None:
                    node_lo(state_f, 2 * p + 1, 1)
                if q is not None:
                    mask(q, 1)
                    moments_of(q, 1, 0)
                    relation_lo(q, 1)
                    normalise(q, 1, 0, normed)
                    norms(q, 1)
                    conv_x_lo(q, 0, 0)
                if p is not None:
                    for k in range(2):
                        a_lo(front, 2 * p + 1, k)
                if q is not None:
                    sum_attended(q, 1)
                    moments_of(q, 1, 1)
                    conv_ax_lo(q, 0, 0)
                    normalise(q, 1, 1, normed)
                if p is not None:
                    reset_arg(front, 2 * p + 1, 0)
                if q is not None:
                    conv_x_lo(q, 0, 1)
                if p is not None:
                    reset_arg(front, 2 * p + 1, 1)
                    reset_h(front, 2 * p + 1, 0)
                if q is not None:
                    sum_conv(q, 0, 0)
                if p is not None:
                    reset_h(front, 2 * p + 1, 1)
                if q is not None:
                    moments_of(q, 2, 0)
                    conv_ax_lo(q, 0, 1)
                if p is not None:
                    for k in range(2):
                        rh_lo(front, 2 * p + 1, k)
                if q is not None:
                    normalise(q, 2, 0, normed)
                    sum_conv(q, 0, 1)
                    moments_of(q, 2, 1)
                    conv_x_lo(q, 1, 0)
                    normalise(q, 2, 1, normed)
                if p is not None:
                    candidate_part(front, 2 * p + 1, 0)
                    hand_over_h(p, 0)
                if q is not None:
                    conv_x_lo(q, 1, 1)
                if p is not None:
                    candidate_part(front, 2 * p + 1, 1)
                    hand_over_h(p, 1)
                if q is not None:
                    conv_ax_lo(q, 1, 0)
                if p is not None:
                    feat_lo(state_b, p, 0)
                if q is not None:
                    conv_ax_lo(q, 1, 1)
                if p is not None:
                    feat_lo(state_b, p, 1)
                if q is not None:
                    sum_conv(q, 1, 0)
                if p is not None:
                    for k in range(2):
                        node_lo(state_b, p, k)
                if q is not None:
                    moments_of(q, 3, 0)
                    sum_conv(q, 1, 1)
                    moments_of(q, 3, 1)
                    for k in range(2):
                        normalise(q, 3, k, result)

            body(0, None)
            body(1, 0)
            with dve.Fori(2, PAIRS) as p:
                body(p, p - 1)
            body(None, LAST)


_INS = ["x", "adj", "L0_gnn_w3_w", "L0_gnn_w3_b", "L0_gnn_u3_w", "L0_gnn_u3_b", "L0_gnn_w4_w", "L0_gnn_w4_b",
        "L0_gnn_w5_w", "L0_gnn_w5_b", "L0_gnn_u5_w", "L0_gnn_u5_b", "L1_gnn_Wq", "L1_gnn_Wk", "L1_gnn_Wv",
        "L2_gnn_weight", "L2_gnn_bias", "L3_gnn_weight", "L3_gnn_bias"]


def kernel(**inputs):
    import numpy as _np
    import concourse.bacc as _bacc
    from concourse.bass_utils import run_bass_kernel_spmd as _run

    nc = _bacc.Bacc("TRN2", target_bir_lowering=False, num_devices=1)
    arrays, args = {}, []
    for name in _INS:
        a = _np.ascontiguousarray(inputs[name])
        arrays[f"in_{name}"] = a
        args.append(nc.dram_tensor(f"in_{name}", a.shape, mybir.dt.from_np(a.dtype), kind="ExternalInput").ap())
    shape = inputs["x"].shape
    args.append(nc.dram_tensor("out_0", shape, F32, kind="ExternalOutput").ap())
    build(nc, *args)
    r = _run(nc, [arrays], core_ids=[0])
    return r.results[0]["out_0"]
```

```python
from contextlib import ExitStack

import concourse.bass as bass
from concourse import mybir

P = 128
F32 = mybir.dt.float32
F32R = mybir.dt.float32r
ALU = mybir.AluOpType
ACT = mybir.ActivationFunctionType
AX = mybir.AxisListType
EPS = 1e-5
TINY = 1.1754944e-38


class Split:

    def __init__(self, hi, lo):
        self.hi, self.lo = hi, lo


class State:

    def __init__(self, sb, sem, name, full, by_graph):
        self.feat = sb(f"{name}_feat", full)
        self.feat_hi, self.feat_lo = sb(f"{name}_feat_hi", full, F32R), sb(f"{name}_feat_lo", full, F32R)
        self.node_hi, self.node_lo = sb(f"{name}_node_hi", by_graph, F32R), sb(f"{name}_node_lo", by_graph, F32R)
        self.s_feat = sem(f"{name}_s_feat")
        self.s_feat_hi, self.s_feat_lo = sem(f"{name}_s_feat_hi"), sem(f"{name}_s_feat_lo")
        self.s_turned = sem(f"{name}_s_turned")
        self.s_node_hi, self.s_node_lo = sem(f"{name}_s_node_hi"), sem(f"{name}_s_node_lo")


class Lane:

    def __init__(self, sb, psum, sem, name, state, full):
        self.state = state
        self.ps0, self.ps1 = psum(f"{name}_ps0", full), psum(f"{name}_ps1", full)
        self.a_hi, self.a_lo = sb(f"{name}_a_hi", full, F32R), sb(f"{name}_a_lo", full, F32R)
        self.gate = sb(f"{name}_gate", full)
        self.rh_hi, self.rh_lo = sb(f"{name}_rh_hi", full, F32R), sb(f"{name}_rh_lo", full, F32R)
        self.z = sb(f"{name}_z", full)
        self.kept = sb(f"{name}_kept", full)
        self.cand = sb(f"{name}_cand", full)
        self.s_mixed = sem("{}_s_mixed".format(name))
        self.s_a_hi = sem("{}_s_a_hi".format(name))
        self.s_a_lo = sem("{}_s_a_lo".format(name))
        self.s_base = sem("{}_s_base".format(name))
        self.s_base_kept = sem("{}_s_base_kept".format(name))
        self.s_reset = sem("{}_s_reset".format(name))
        self.s_reset_arg = sem("{}_s_reset_arg".format(name))
        self.s_r = sem("{}_s_r".format(name))
        self.s_rh = sem("{}_s_rh".format(name))
        self.s_rh_hi = sem("{}_s_rh_hi".format(name))
        self.s_rh_lo = sem("{}_s_rh_lo".format(name))
        self.s_update = sem("{}_s_update".format(name))
        self.s_z = sem("{}_s_z".format(name))
        self.s_omz = sem("{}_s_omz".format(name))
        self.s_kept = sem("{}_s_kept".format(name))
        self.s_cand = sem("{}_s_cand".format(name))
        self.s_tanh = sem("{}_s_tanh".format(name))
        self.s_zc = sem("{}_s_zc".format(name))


class Layers:

    def __init__(self, sb, sem, name, lane, per_graph, x, s_x, x_before, summed, normed, skip, result, v, rel_split,
                 sq_sum):
        self.ps0, self.ps1 = lane.ps0, lane.ps1
        self.x, self.s_x, self.x_before = x, s_x, x_before
        self.h3 = lane.cand
        self.summed = summed
        self.normed = normed
        self.skip = skip
        self.result = result
        self.x_hi, self.x_lo = per_graph(lane.a_hi), per_graph(lane.a_lo)
        self.y_hi, self.y_lo = per_graph(lane.rh_hi), per_graph(lane.rh_lo)
        self.v_hi, self.v_lo = v
        self.rel, self.rel_sq = per_graph(lane.gate), per_graph(lane.z)
        self.rel_hi, self.rel_lo = rel_split
        self.sq_sum = sq_sum
        G, N = sq_sum.shape[1:]
        C = N // P
        self.sq_hi, self.sq_lo = sb(name + "_sq_hi", [P, G, N], F32R), sb(name + "_sq_lo", [P, G, N], F32R)
        self.stats = sb(name + "_stats", [P, G, C, 6])
        self.moments = sb(name + "_moments", [P, G, C, 2])
        self.var_eps = sb(name + "_var_eps", [P, G, C])
        self.pad = sb(name + "_pad", [P, G])
        self.rstd = sb(name + "_rstd", [P, G, C])
        self.norm_sq = sb(name + "_norm_sq", [P, G, C])
        self.norm_inv = sb(name + "_norm_inv", [P, G, C])
        self.s_h3 = sem(name + "_layer_h3")
        self.s_h3_turned = sem(name + "_layer_h3_turned")
        self.s_sum = sem(name + "_layer_sum")
        self.s_stats = sem(name + "_layer_stats")
        self.s_moments = sem(name + "_layer_moments")
        self.s_var = sem(name + "_layer_var")
        self.s_rstd = sem(name + "_layer_rstd")
        self.s_normed = sem(name + "_layer_normed")
        self.s_x1_turned = sem(name + "_layer_x1_turned")
        self.s_x1_hi = sem(name + "_layer_x1_hi")
        self.s_x1_lo = sem(name + "_layer_x1_lo")
        self.s_y = sem(name + "_layer_y")
        self.s_y_hi = sem(name + "_layer_y_hi")
        self.s_y_lo = sem(name + "_layer_y_lo")
        self.s_v = sem(name + "_layer_v")
        self.s_v_hi = sem(name + "_layer_v_hi")
        self.s_v_lo = sem(name + "_layer_v_lo")
        self.s_rel = sem(name + "_layer_rel")
        self.s_masked = sem(name + "_layer_masked")
        self.s_rel_hi = sem(name + "_layer_rel_hi")
        self.s_rel_lo = sem(name + "_layer_rel_lo")
        self.s_rel_sq = sem(name + "_layer_rel_sq")
        self.s_sq_sum = sem(name + "_layer_sq_sum")
        self.s_sq_hi = sem(name + "_layer_sq_hi")
        self.s_sq_lo = sem(name + "_layer_sq_lo")
        self.s_norm = sem(name + "_layer_norm")
        self.s_norm_sq = sem(name + "_layer_norm_sq")
        self.s_norm_inv = sem(name + "_layer_norm_inv")
        self.s_attended = sem(name + "_layer_attended")
        self.s_x_hi = sem(name + "_layer_x_hi")
        self.s_x_lo = sem(name + "_layer_x_lo")
        self.s_skip = sem(name + "_layer_skip")
        self.s_ax = sem(name + "_layer_ax")
        self.s_ax_hi = sem(name + "_layer_ax_hi")
        self.s_ax_lo = sem(name + "_layer_ax_lo")
        self.s_conv = sem(name + "_layer_conv")


def build(nc, x, adj, w3_w, w3_b, u3_w, u3_b, w4_w, w4_b, w5_w, w5_b, u5_w, u5_b, wq, wk, wv,
          l2_w, l2_b, l3_w, l3_b, out):
    B, N, D = x.shape
    C = N // P
    G = 2
    T = G * N
    PAIRS = B // G
    assert N == D and C == 2 and T == 512
    LAST = PAIRS - 1

    x_pairs = x.rearrange("(q g) (c p) d -> q p g c d", g=G, p=P)
    out_pairs = out.rearrange("(q g) (c p) d -> q p g c d", g=G, p=P)

    with ExitStack() as ctx:
        def sb(name, shape, dt=F32):
            return ctx.enter_context(nc.sbuf_tensor(name, shape, dt))

        def sem(name):
            return ctx.enter_context(nc.semaphore(name))

        def split_matrix(name):
            return Split(sb(name + "_hi", [P, C, D], F32R), sb(name + "_lo", [P, C, D], F32R))

        adjT = split_matrix("adjT")
        norm_adjT = split_matrix("norm_adjT")
        w3T = split_matrix("w3T")
        w4T = split_matrix("w4T")
        w5T = split_matrix("w5T")
        u3T = split_matrix("u3T")
        u5T = split_matrix("u5T")
        wvT = split_matrix("wvT")
        wqk = split_matrix("wqk")
        w2s = split_matrix("w2s")
        w3s = split_matrix("w3s")

        ident = sb("ident", [P, P])
        adj_nat = sb("adj_nat", [P, C, N])
        ones = sb("ones", [P, 2], F32R)
        eps = sb("eps", [P, C])
        neg_half = sb("neg_half", [P, C])
        bias_in = sb("bias_in", [P, 5, C])
        bias_z = sb("bias_z", [P, C])
        neg_bias_z = sb("neg_bias_z", [P, C])
        bias_r = sb("bias_r", [P, C])
        bias_c = sb("bias_c", [P, C])
        bias_out = sb("bias_out", [P, 2, C, D])
        deg = sb("deg", [P, C])
        deg_floor = sb("deg_floor", [P, C])
        deg_pos = sb("deg_pos", [P, C])
        deg_pow = sb("deg_pow", [P, C])
        deg_inv = sb("deg_inv", [P, C])

        def psum(name, shape):
            return ctx.enter_context(nc.psum_tensor(name, shape, F32))

        state_f = State(sb, sem, "hf", [P, C, T], [P, G, C, D])
        state_b = State(sb, sem, "hb", [P, C, T], [P, G, C, D])
        front = Lane(sb, psum, sem, "f", state_f, [P, C, T])
        back = Lane(sb, psum, sem, "b", state_b, [P, C, T])

        def per_graph(t):
            return t[:].rearrange("p c (k n) -> p c k n", k=C)

        x_front = sb("x_front", [P, G, C, D])
        x_back = sb("x_back", [P, G, C, D])
        s_x_front, s_x_back = sem("s_x_front"), sem("s_x_back")

        def nodes(name, dt=F32):
            return sb(name, [P, G, C, D], dt)

        main = Layers(sb, sem, "b", back, per_graph, x_back, s_x_back, 0,
                      nodes("summed"), nodes("normed"), nodes("skip"), nodes("result"),
                      (nodes("v_hi", F32R), nodes("v_lo", F32R)), (nodes("rel_hi", F32R), nodes("rel_lo", F32R)),
                      sb("sq_sum", [P, G, N]))
        last_pair = Layers(sb, sem, "f", front, per_graph, x_front, s_x_front, LAST,
                           per_graph(front.kept), per_graph(state_f.feat), x_front, per_graph(front.gate),
                           (per_graph(state_f.feat_hi), per_graph(state_f.feat_lo)), (state_f.node_hi, state_f.node_lo),
                           front.cand[:, 0, :].rearrange("p (g n) -> p g n", g=G))

        w3_nat, w4_nat, w5_nat = back.gate[:], back.z[:], back.kept[:]
        flat = lambda t: t[:].rearrange("p g c d -> p (g c) d")
        u3_nat, u5_nat = flat(x_back)[:, 0:C], flat(x_back)[:, C:2 * C]
        wq_nat, wk_nat = flat(main.summed)[:, 0:C], flat(main.summed)[:, C:2 * C]
        wv_nat, w2_nat = flat(main.normed)[:, 0:C], flat(main.normed)[:, C:2 * C]
        w3s_nat = flat(main.skip)[:, 0:C]
        adj_rows, norm_full = flat(main.result)[:, 0:C], flat(main.result)[:, C:2 * C]

        s_stored = sem("s_stored")
        s_load = {n: sem("s_load_" + n) for n in ("adj", "u3", "w4", "w3", "w5", "u5", "qk", "v", "l23", "bias", "bias_out")}
        s_consts, s_bias, s_halves = sem("s_consts"), sem("s_bias"), sem("s_halves")
        s_deg, s_deg_pow, s_rows, s_norm_full = sem("s_deg"), sem("s_deg_pow"), sem("s_rows"), sem("s_norm_full")
        s_prep, s_prep_hi, s_prep_lo = sem("s_prep"), sem("s_prep_hi"), sem("s_prep_lo")
        s_in_turned = sem("s_in_turned")

        def upto(n, k=1):
            return 2 * n + k + 1

        def ln(q, j, g):
            return 8 * q + 2 * j + g + 1

        def conv(q, j, g=1):
            return 4 * q + 2 * j + g + 1

        prepared = [adjT, u3T, w4T, w3T, w5T, u5T, wvT, wqk, norm_adjT]

        def prep_bank(i):
            ps = (back.ps0, back.ps1)[i // 2 % 2]
            return ps[:, i % 2, :].rearrange("p (c n) -> p c n", c=C)

        def later(n):
            return not (isinstance(n, int) and n == 0)

        block = ctx.enter_context(nc.Block())

        @block.sync
        def _(sp):
            def rows(w):
                return w.rearrange("(c p) d -> p c d", p=P)

            sp.dma_start(adj_nat[:], rows(adj)).then_inc(s_load["adj"], 16)
            sp.dma_start(x_front[:], x_pairs[0]).then_inc(s_x_front, 16)
            sp.dma_start(u3_nat, rows(u3_w)).then_inc(s_load["u3"], 16)
            sp.dma_start(w4_nat, rows(w4_w)).then_inc(s_load["w4"], 16)
            sp.dma_start(w3_nat, rows(w3_w)).then_inc(s_load["w3"], 16)
            sp.dma_start(w5_nat, rows(w5_w)).then_inc(s_load["w5"], 16)
            sp.dma_start(u5_nat, rows(u5_w)).then_inc(s_load["u5"], 16)
            sp.dma_start(wv_nat, rows(wv)).then_inc(s_load["v"], 16)
            sp.dma_start(wq_nat, rows(wq)).then_inc(s_load["qk"], 16)
            sp.dma_start(wk_nat, rows(wk)).then_inc(s_load["qk"], 16)
            sp.dma_start(w2_nat, rows(l2_w)).then_inc(s_load["l23"], 16)
            sp.dma_start(w3s_nat, rows(l3_w)).then_inc(s_load["l23"], 16)

            def load_front(p):
                sp.wait_ge(s_in_turned, upto(p - 1))
                sp.wait_ge(state_f.s_node_lo, upto(2 * p - 2))
                sp.dma_start(x_front[:], x_pairs[p]).then_inc(s_x_front, 16)

            def load_back(q):
                sp.wait_ge(main.s_sum, ln(q - 1, 0, 1))
                sp.dma_start(x_back[:], x_pairs[q]).then_inc(s_x_back, 16)

            def store(Y, q):
                sp.wait_ge(Y.s_normed, ln(q, 3, 1))
                sp.dma_start(out_pairs[q + Y.x_before], Y.result[:]).then_inc(s_stored, 16)

            load_front(1)
            sp.wait_ge(s_prep, 6)
            sp.dma_start(x_back[:], x_pairs[0]).then_inc(s_x_back, 16)
            with sp.Fori(1, LAST) as p:
                load_front(p + 1)
                load_back(p)
                store(main, p - 1)
            store(main, LAST - 1)
            store(last_pair, 0)
            sp.wait_ge(s_stored, 16 * PAIRS)

        @block.gpsimd
        def _(pool):
            pool.memset(ident[:], 0.0).then_inc(s_consts, 1)
            pool.memset(ones[:].bitcast(F32), 1.0).then_inc(s_consts, 1)
            pool.memset(neg_half[:], -0.5).then_inc(s_consts, 1)
            pool.memset(eps[:], EPS).then_inc(s_consts, 1)
            pool.wait_ge(s_consts, 4)
            pool.affine_select(out=ident[:], in_=ident[:], compare_op=ALU.not_equal, fill=1.0, base=0,
                               pattern=[[-1, P]], channel_multiplier=1).then_inc(s_consts, 1)

            def input_nodes_lo(p, g):
                pool.wait_ge(state_f.s_node_hi, upto(2 * p, g))
                pool.tensor_tensor(state_f.node_lo[:, g], x_front[:, g], state_f.node_hi[:, g].bitcast(F32),
                                   ALU.subtract).then_inc(state_f.s_node_lo, 1)

            def input_lo(p, k):
                pool.wait_ge(state_f.s_feat, upto(2 * p, k))
                pool.tensor_tensor(state_f.feat_lo[:, k], state_f.feat[:, k], state_f.feat_hi[:, k].bitcast(F32),
                                   ALU.subtract).then_inc(state_f.s_feat_lo, 1)

            def keep(L, n, k):
                pool.wait_ge(L.state.s_feat, upto(n, k))
                pool.wait_ge(L.s_omz, upto(n, k))
                pool.tensor_tensor(L.kept[:, k], L.kept[:, k], L.state.feat[:, k], ALU.mult).then_inc(L.s_kept, 1)

            def squares_sum(Y, q, g):
                pool.wait_ge(Y.s_rel_sq, upto(q, g))
                pool.tensor_tensor(Y.sq_sum[:, g], Y.rel_sq[:, g, 0], Y.rel_sq[:, g, 1], ALU.add).then_inc(Y.s_sq_sum, 1)

            def squares_lo(Y, q, g):
                pool.wait_ge(Y.s_sq_hi, upto(q, g))
                pool.tensor_tensor(Y.sq_lo[:, g], Y.sq_sum[:, g], Y.sq_hi[:, g].bitcast(F32),
                                   ALU.subtract).then_inc(Y.s_sq_lo, 1)

            def inverse_std(Y, q, j, g):
                pool.wait_ge(Y.s_moments, ln(q, j, g))
                pool.tensor_tensor(Y.var_eps[:, g], Y.moments[:, g, :, 1], eps[:], ALU.add).then_inc(Y.s_var, 1)
                pool.wait_ge(Y.s_var, ln(q, j, g))
                pool.tensor_tensor(Y.rstd[:, g], Y.var_eps[:, g], neg_half[:], ALU.pow).then_inc(Y.s_rstd, 1)

            def inverse_norm(Y, q, g):
                pool.wait_ge(Y.s_norm_sq, upto(q, g))
                pool.tensor_tensor(Y.norm_inv[:, g], Y.norm_sq[:, g], neg_half[:], ALU.pow).then_inc(Y.s_norm_inv, 1)

            def add_bias(Y, q, j, g):
                pool.wait_ge(Y.s_normed, ln(q, j + 1, g))
                pool.tensor_tensor(Y.skip[:, g], Y.normed[:, g], bias_out[:, j], ALU.add).then_inc(Y.s_skip, 1)

            def body(p, q):
                input_nodes_lo(p, 0)
                keep(back, q, 0)
                input_lo(p, 0)
                input_nodes_lo(p, 1)
                input_lo(p, 1)
                keep(back, q, 1)
                for k in range(2):
                    inverse_std(main, q, 0, k)
                for k in range(2):
                    keep(front, 2 * p, k)
                squares_sum(main, q, 0)
                squares_lo(main, q, 0)
                squares_sum(main, q, 1)
                inverse_norm(main, q, 0)
                squares_lo(main, q, 1)
                inverse_norm(main, q, 1)
                for k in range(2):
                    inverse_std(main, q, 1, k)
                for k in range(2):
                    add_bias(main, q, 0, k)
                keep(front, 2 * p + 1, 0)
                for k in range(2):
                    inverse_std(main, q, 2, k)
                add_bias(main, q, 1, 0)
                keep(front, 2 * p + 1, 1)
                add_bias(main, q, 1, 1)
                for k in range(2):
                    inverse_std(main, q, 3, k)

            def finish():
                for k in range(2):
                    input_nodes_lo(LAST, k)
                for k in range(2):
                    input_lo(LAST, k)
                for k in range(2):
                    keep(front, 2 * LAST, k)
                for k in range(2):
                    keep(front, 2 * LAST + 1, k)
                for k in range(2):
                    keep(back, LAST - 1, k)
                inverse_std(main, LAST - 1, 0, 0)
                keep(front, 2 * LAST + 2, 0)
                inverse_std(main, LAST - 1, 0, 1)
                keep(front, 2 * LAST + 2, 1)
                for k in range(2):
                    inverse_std(last_pair, 0, 0, k)
                squares_sum(main, LAST - 1, 0)
                squares_lo(main, LAST - 1, 0)
                squares_sum(main, LAST - 1, 1)
                squares_sum(last_pair, 0, 0)
                inverse_norm(main, LAST - 1, 0)
                squares_lo(last_pair, 0, 0)
                inverse_norm(last_pair, 0, 0)
                squares_lo(main, LAST - 1, 1)
                inverse_std(main, LAST - 1, 1, 0)
                inverse_std(last_pair, 0, 1, 0)
                squares_sum(last_pair, 0, 1)
                inverse_norm(main, LAST - 1, 1)
                squares_lo(last_pair, 0, 1)
                add_bias(main, LAST - 1, 0, 0)
                inverse_norm(last_pair, 0, 1)
                add_bias(last_pair, 0, 0, 0)
                inverse_std(main, LAST - 1, 1, 1)
                inverse_std(last_pair, 0, 1, 1)
                add_bias(main, LAST - 1, 0, 1)
                inverse_std(last_pair, 0, 2, 0)
                inverse_std(main, LAST - 1, 2, 0)
                add_bias(last_pair, 0, 0, 1)
                add_bias(last_pair, 0, 1, 0)
                add_bias(main, LAST - 1, 1, 0)
                inverse_std(last_pair, 0, 2, 1)
                inverse_std(main, LAST - 1, 2, 1)
                add_bias(main, LAST - 1, 1, 1)
                add_bias(last_pair, 0, 1, 1)
                inverse_std(main, LAST - 1, 3, 0)
                for k in range(2):
                    inverse_std(last_pair, 0, 3, k)
                inverse_std(main, LAST - 1, 3, 1)

            for i, b in enumerate((l2_b, l3_b)):
                for c in range(C):
                    pool.dma_start(bias_out[:, i, c, :], b.partition_broadcast(P)).then_inc(s_load["bias_out"], 16)
            pool.wait_ge(s_deg, 3)
            pool.tensor_tensor(deg_pow[:], deg_floor[:], neg_half[:], ALU.pow).then_inc(s_deg_pow, 1)
            for n in range(2):
                for k in range(C):
                    keep(front, n, k)
            pool.wait_ge(s_load["bias_out"], 16 * 2 * C)
            body(1, 0)
            with pool.Fori(2, LAST) as p:
                body(p, p - 1)
            finish()

        @block.tensor
        def _(pe):
            def product(bank, stationary, moving, start=True, stop=True):
                terms = [(s, m) for (sh, sl), (mh, ml) in zip(stationary, moving)
                         for s, m in ((sh, mh), (sh, ml), (sl, mh))]
                for i, (s, m) in enumerate(terms):
                    last = pe.matmul(bank, s, m, start=start and i == 0, stop=stop and i == len(terms) - 1,
                                     skip_group_check=True)
                return last

            def columns(m, k):
                return [(m.hi[:, c, k * P:(k + 1) * P], m.lo[:, c, k * P:(k + 1) * P]) for c in range(C)]

            def whole(m):
                return [(m.hi[:, c, :], m.lo[:, c, :]) for c in range(C)]

            def graph_columns(hi, lo, g, k):
                return [(hi[:, g, c, k * P:(k + 1) * P], lo[:, g, c, k * P:(k + 1) * P]) for c in range(C)]

            def graph_whole(hi, lo, g):
                return [(hi[:, g, c, :], lo[:, g, c, :]) for c in range(C)]

            def turn_matrix(i, src):
                bank = prep_bank(i)
                for k in range(C):
                    for c in range(C):
                        last = pe.transpose(bank[:, k, c * P:(c + 1) * P], src[:, c, k * P:(k + 1) * P], ident[:])
                last.then_inc(s_prep, 1)

            def query_key_matrix():
                bank = prep_bank(7)
                for k in range(C):
                    for c in range(C):
                        last = pe.matmul(bank[:, k, :], wq_nat[:, c, k * P:(k + 1) * P], wk_nat[:, c, :],
                                         start=c == 0, stop=c == C - 1)
                last.then_inc(s_prep, 1)

            def turn_input(p, k):
                pe.wait_ge(s_x_front, 16 * p + 16)
                if later(p):
                    pe.wait_ge(front.s_z, upto(2 * p - 1, k))
                    pe.wait_ge(front.s_omz, upto(2 * p - 1, k))
                for g in range(G):
                    for c in range(C):
                        last = pe.transpose(front.ps0[:, k, g * N + c * P:g * N + (c + 1) * P],
                                            x_front[:, g, c, k * P:(k + 1) * P], ident[:])
                last.then_inc(s_in_turned, 1)

            def mix(L, n, k, pair=None):
                S = L.state
                pe.wait_ge(S.s_node_lo, upto(n))
                if L is back and later(n):
                    pe.wait_ge(main.s_ax_lo, conv(n - 1, 1, k))
                if pair is not None and later(pair):
                    pe.wait_ge(state_b.s_node_lo, upto(pair - 1, k))
                for g in range(G):
                    last = product(L.ps1[:, k, g * N:(g + 1) * N],
                                   graph_columns(S.node_hi, S.node_lo, g, k), whole(adjT))
                last.then_inc(L.s_mixed, 1)

            def base(L, n, k):
                S = L.state
                pe.wait_ge(S.s_feat_lo, upto(n))
                if L is back and later(n):
                    pe.wait_ge(main.s_sum, ln(n - 1, 3, k))
                product(L.ps0[:, k], columns(u3T, k),
                        [(S.feat_hi[:, c], S.feat_lo[:, c]) for c in range(C)]).then_inc(L.s_base, 1)

            def mixed(L):
                return [(L.a_hi[:, c], L.a_lo[:, c]) for c in range(C)]

            def reset(L, n, k):
                pe.wait_ge(L.s_a_lo, upto(n))
                product(L.ps1[:, k], columns(w4T, k), mixed(L)).then_inc(L.s_reset, 1)

            def update(L, n, k):
                pe.wait_ge(L.s_a_lo, upto(n))
                pe.wait_ge(L.s_base_kept, upto(n, k))
                product(L.ps0[:, k], columns(w3T, k), mixed(L), start=False).then_inc(L.s_update, 1)

            def candidate_mixed(L, n, k):
                pe.wait_ge(L.s_reset_arg, upto(n, k))
                product(L.ps1[:, k], columns(w5T, k), mixed(L), stop=False)

            def candidate_reset(L, n, k):
                pe.wait_ge(L.s_rh_lo, upto(n))
                product(L.ps1[:, k], columns(u5T, k), [(L.rh_hi[:, c], L.rh_lo[:, c]) for c in range(C)],
                        start=False).then_inc(L.s_cand, 1)

            def turn(ps1, g, feat, done):
                for c in range(C):
                    for k in range(C):
                        last = pe.transpose(ps1[:, g, c * D + k * P:c * D + (k + 1) * P],
                                            feat[:, k, g * N + c * P:g * N + (c + 1) * P], ident[:])
                last.then_inc(done, 1)

            def turn_h(S, v, g):
                pe.wait_ge(S.s_feat, upto(v))
                turn(front.ps1, g, S.feat, S.s_turned)

            def turn_h3(Y, q, g):
                pe.wait_ge(Y.s_h3, upto(q))
                turn(Y.ps1, g, Y.h3, Y.s_h3_turned)

            def turn_x1(Y, q, g):
                pe.wait_ge(Y.s_normed, ln(q, 0, g))
                for k in range(C):
                    for c in range(C):
                        last = pe.transpose(Y.ps1[:, g, k * N + c * P:k * N + (c + 1) * P],
                                            Y.normed[:, g, c, k * P:(k + 1) * P], ident[:])
                last.then_inc(Y.s_x1_turned, 1)

            def keys(Y, q, g):
                pe.wait_ge(Y.s_x1_lo, upto(q, g))
                for k in range(C):
                    last = product(Y.ps0[:, g, k * N:(k + 1) * N], columns(wqk, k), graph_whole(Y.x_hi, Y.x_lo, g))
                last.then_inc(Y.s_y, 1)

            def values(Y, q, g):
                pe.wait_ge(Y.s_x1_lo, upto(q, g))
                for c in range(C):
                    last = product(Y.ps1[:, g, c * D:(c + 1) * D], graph_columns(Y.x_hi, Y.x_lo, g, c), whole(wvT))
                last.then_inc(Y.s_v, 1)

            def relate(Y, q, g):
                pe.wait_ge(Y.s_y_lo, upto(q, g))
                for c in range(C):
                    last = product(Y.ps0[:, g, c * N:(c + 1) * N], graph_columns(Y.x_hi, Y.x_lo, g, c),
                                   graph_whole(Y.y_hi, Y.y_lo, g))
                last.then_inc(Y.s_rel, 1)

            def sum_squares(Y, q, g):
                pe.wait_ge(Y.s_v_lo, upto(q, g))
                pe.wait_ge(Y.s_sq_lo, upto(q, g))
                for c in range(C):
                    for part in (Y.sq_hi, Y.sq_lo):
                        last = pe.matmul(Y.ps1[:, g, 2 * c:2 * c + 2], part[:, g, c * P:(c + 1) * P], ones[:],
                                         start=part is Y.sq_hi, stop=part is Y.sq_lo, skip_group_check=True)
                last.then_inc(Y.s_norm, 1)

            def attend(Y, q, g):
                pe.wait_ge(Y.s_v_lo, upto(q, g))
                pe.wait_ge(Y.s_rel_lo, upto(q, g))
                for c in range(C):
                    last = product(Y.ps0[:, g, c * D:(c + 1) * D], graph_columns(Y.rel_hi, Y.rel_lo, g, c),
                                   graph_whole(Y.v_hi, Y.v_lo, g))
                last.then_inc(Y.s_attended, 1)

            def mix_nodes(Y, q, j, g):
                pe.wait_ge(Y.s_x_lo, conv(q, j, g))
                if j == 0:
                    pe.wait_ge(Y.s_norm_sq, upto(q, g))
                for k in range(C):
                    last = product(Y.ps1[:, g, k * N:(k + 1) * N], graph_columns(Y.x_hi, Y.x_lo, g, k),
                                   whole((adjT, norm_adjT)[j]))
                last.then_inc(Y.s_ax, 1)

            def convolve(Y, q, j, g):
                pe.wait_ge(Y.s_ax_lo, conv(q, j, g))
                for c in range(C):
                    last = product(Y.ps0[:, g, c * D:(c + 1) * D], graph_columns(Y.y_hi, Y.y_lo, g, c),
                                   whole((w2s, w3s)[j]))
                last.then_inc(Y.s_conv, 1)

            def body(p, q):
                for k in range(2):
                    turn_input(p, k)
                for k in range(2):
                    mix(back, q, k)
                for k in range(2):
                    base(back, q, k)
                for k in range(2):
                    reset(back, q, k)
                update(back, q, 0)
                candidate_mixed(back, q, 0)
                update(back, q, 1)
                candidate_mixed(back, q, 1)
                for k in range(2):
                    candidate_reset(back, q, k)
                for k in range(2):
                    mix(front, 2 * p, k, p)
                base(front, 2 * p, 0)
                turn_h3(main, q, 0)
                base(front, 2 * p, 1)
                turn_h3(main, q, 1)
                for k in range(2):
                    reset(front, 2 * p, k)
                for k in range(2):
                    update(front, 2 * p, k)
                candidate_mixed(front, 2 * p, 0)
                turn_x1(main, q, 0)
                candidate_mixed(front, 2 * p, 1)
                turn_x1(main, q, 1)
                candidate_reset(front, 2 * p, 0)
                for k in range(2):
                    keys(main, q, k)
                candidate_reset(front, 2 * p, 1)
                relate(main, q, 0)
                values(main, q, 0)
                relate(main, q, 1)
                for k in range(2):
                    turn_h(state_f, 2 * p + 1, k)
                values(main, q, 1)
                sum_squares(main, q, 0)
                attend(main, q, 0)
                mix(front, 2 * p + 1, 0)
                sum_squares(main, q, 1)
                mix(front, 2 * p + 1, 1)
                attend(main, q, 1)
                base(front, 2 * p + 1, 0)
                reset(front, 2 * p + 1, 0)
                base(front, 2 * p + 1, 1)
                reset(front, 2 * p + 1, 1)
                mix_nodes(main, q, 0, 0)
                update(front, 2 * p + 1, 0)
                mix_nodes(main, q, 0, 1)
                convolve(main, q, 0, 0)
                candidate_mixed(front, 2 * p + 1, 0)
                convolve(main, q, 0, 1)
                candidate_reset(front, 2 * p + 1, 0)
                update(front, 2 * p + 1, 1)
                candidate_mixed(front, 2 * p + 1, 1)
                candidate_reset(front, 2 * p + 1, 1)
                for k in range(2):
                    mix_nodes(main, q, 1, k)
                for k in range(2):
                    turn_h(state_b, p, k)
                for k in range(2):
                    convolve(main, q, 1, k)

            def finish():
                turn_input(LAST, 0)
                mix(back, LAST - 1, 0)
                turn_input(LAST, 1)
                base(back, LAST - 1, 0)
                mix(back, LAST - 1, 1)
                for k in range(2):
                    mix(front, 2 * LAST, k, LAST)
                for k in range(2):
                    base(front, 2 * LAST, k)
                for k in range(2):
                    reset(front, 2 * LAST, k)
                candidate_mixed(front, 2 * LAST, 0)
                update(front, 2 * LAST, 0)
                reset(back, LAST - 1, 0)
                update(front, 2 * LAST, 1)
                candidate_reset(front, 2 * LAST, 0)
                candidate_mixed(front, 2 * LAST, 1)
                candidate_reset(front, 2 * LAST, 1)
                reset(back, LAST - 1, 1)
                base(back, LAST - 1, 1)
                for k in range(2):
                    turn_h(state_f, 2 * LAST + 1, k)
                update(back, LAST - 1, 0)
                base(front, 2 * LAST + 1, 0)
                for k in range(2):
                    mix(front, 2 * LAST + 1, k)
                update(back, LAST - 1, 1)
                base(front, 2 * LAST + 1, 1)
                for k in range(2):
                    reset(front, 2 * LAST + 1, k)
                candidate_mixed(front, 2 * LAST + 1, 0)
                for k in range(2):
                    update(front, 2 * LAST + 1, k)
                candidate_mixed(front, 2 * LAST + 1, 1)
                for k in range(2):
                    candidate_reset(front, 2 * LAST + 1, k)
                for k in range(2):
                    candidate_mixed(back, LAST - 1, k)
                for k in range(2):
                    turn_h(state_f, 2 * LAST + 2, k)
                for k in range(2):
                    candidate_reset(back, LAST - 1, k)
                for k in range(2):
                    mix(front, 2 * LAST + 2, k)
                base(front, 2 * LAST + 2, 0)
                for k in range(2):
                    turn_h3(main, LAST - 1, k)
                base(front, 2 * LAST + 2, 1)
                for k in range(2):
                    reset(front, 2 * LAST + 2, k)
                for k in range(2):
                    update(front, 2 * LAST + 2, k)
                candidate_mixed(front, 2 * LAST + 2, 0)
                turn_x1(main, LAST - 1, 0)
                candidate_mixed(front, 2 * LAST + 2, 1)
                for k in range(2):
                    candidate_reset(front, 2 * LAST + 2, k)
                keys(main, LAST - 1, 0)
                turn_x1(main, LAST - 1, 1)
                for k in range(2):
                    turn_h3(last_pair, 0, k)
                values(main, LAST - 1, 0)
                keys(main, LAST - 1, 1)
                values(main, LAST - 1, 1)
                turn_x1(last_pair, 0, 0)
                for k in range(2):
                    relate(main, LAST - 1, k)
                keys(last_pair, 0, 0)
                values(last_pair, 0, 0)
                relate(last_pair, 0, 0)
                turn_x1(last_pair, 0, 1)
                sum_squares(main, LAST - 1, 0)
                attend(main, LAST - 1, 0)
                keys(last_pair, 0, 1)
                sum_squares(last_pair, 0, 0)
                attend(last_pair, 0, 0)
                relate(last_pair, 0, 1)
                values(last_pair, 0, 1)
                sum_squares(main, LAST - 1, 1)
                attend(main, LAST - 1, 1)
                sum_squares(last_pair, 0, 1)
                attend(last_pair, 0, 1)
                mix_nodes(last_pair, 0, 0, 0)
                mix_nodes(main, LAST - 1, 0, 0)
                convolve(last_pair, 0, 0, 0)
                convolve(main, LAST - 1, 0, 0)
                mix_nodes(main, LAST - 1, 0, 1)
                mix_nodes(last_pair, 0, 0, 1)
                convolve(main, LAST - 1, 0, 1)
                convolve(last_pair, 0, 0, 1)
                mix_nodes(last_pair, 0, 1, 0)
                mix_nodes(main, LAST - 1, 1, 0)
                convolve(last_pair, 0, 1, 0)
                convolve(main, LAST - 1, 1, 0)
                mix_nodes(last_pair, 0, 1, 1)
                mix_nodes(main, LAST - 1, 1, 1)
                convolve(last_pair, 0, 1, 1)
                convolve(main, LAST - 1, 1, 1)

            pe.wait_ge(s_consts, 5)
            pe.wait_ge(s_load["adj"], 16)
            turn_matrix(0, adj_nat)
            for k in range(C):
                turn_input(0, k)
            pe.wait_ge(s_load["u3"], 16)
            turn_matrix(1, u3_nat)
            pe.wait_ge(s_prep_lo, 1)
            for k in range(C):
                mix(front, 0, k)
            pe.wait_ge(s_halves, 1)
            turn_matrix(2, w4_nat)
            pe.wait_ge(s_prep_lo, 2)
            for k in range(C):
                base(front, 0, k)
            pe.wait_ge(s_halves, 2)
            turn_matrix(3, w3_nat)
            pe.wait_ge(s_halves, 3)
            turn_matrix(4, w5_nat)
            pe.wait_ge(s_load["u5"], 16)
            turn_matrix(5, u5_nat)
            pe.wait_ge(s_prep_lo, 3)
            for k in range(C):
                reset(front, 0, k)
            pe.wait_ge(s_prep_lo, 5)
            for k in range(C):
                update(front, 0, k)
            for k in range(C):
                candidate_mixed(front, 0, k)
            pe.wait_ge(s_prep_lo, 6)
            for k in range(C):
                candidate_reset(front, 0, k)
            pe.wait_ge(s_load["v"], 16)
            turn_matrix(6, wv_nat)
            pe.wait_ge(s_load["qk"], 32)
            query_key_matrix()
            for g in range(G):
                turn_h(state_f, 1, g)
            for k in range(C):
                base(front, 1, k)
            for k in range(C):
                mix(front, 1, k)
            pe.wait_ge(s_rows, 1)
            turn_matrix(8, adj_rows)
            for k in range(C):
                reset(front, 1, k)
            for k in range(C):
                update(front, 1, k)
            for k in range(C):
                candidate_mixed(front, 1, k)
            for k in range(C):
                candidate_reset(front, 1, k)
            for g in range(G):
                turn_h(state_b, 0, g)
            pe.wait_ge(s_prep_lo, len(prepared) + 2)
            body(1, 0)
            with pe.Fori(2, LAST) as p:
                body(p, p - 1)
            finish()

        @block.scalar
        def _(act):
            def copy(dst, src):
                return act.activation(dst, src, ACT.Copy)

            for i, b in enumerate((w3_b, u3_b, w4_b, w5_b, u5_b)):
                act.dma_start(bias_in[:, i, :], b.rearrange("(c p) -> p c", p=P),
                              allow_slow_non_contiguous=True).then_inc(s_load["bias"], 16)

            def prep_hi(i):
                act.wait_ge(s_prep, i + 1)
                copy(prepared[i].hi[:], prep_bank(i)).then_inc(s_prep_hi, 1)

            def input_nodes_hi(p, g):
                act.wait_ge(s_x_front, 16 * p + 16)
                if later(p):
                    act.wait_ge(front.s_mixed, upto(2 * p - 1))
                copy(state_f.node_hi[:, g], x_front[:, g]).then_inc(state_f.s_node_hi, 1)

            def input_hi(p, k):
                if later(p):
                    act.wait_ge(front.s_base, upto(2 * p - 1))
                    act.wait_ge(front.s_kept, upto(2 * p - 1))
                    act.wait_ge(front.s_rh, upto(2 * p - 1))
                act.wait_ge(s_in_turned, upto(p, k))
                copy(state_f.feat_hi[:, k], front.ps0[:, k]).then_inc(state_f.s_feat_hi, 1)
                copy(state_f.feat[:, k], front.ps0[:, k]).then_inc(state_f.s_feat, 1)

            def a_hi(L, n, k):
                act.wait_ge(L.s_mixed, upto(n, k))
                copy(L.a_hi[:, k], L.ps1[:, k]).then_inc(L.s_a_hi, 1)

            def keep_base(L, n, k):
                act.wait_ge(L.s_base, upto(n, k))
                act.activation(L.gate[:, k], L.ps0[:, k], ACT.Identity, bias=bias_r[:, k:k + 1]).then_inc(L.s_base_kept, 1)

            def reset_gate(L, n, k):
                act.wait_ge(L.s_reset_arg, upto(n, k))
                act.activation(L.gate[:, k], L.gate[:, k], ACT.Sigmoid).then_inc(L.s_r, 1)

            def rh_hi(L, n, k):
                act.wait_ge(L.s_rh, upto(n, k))
                copy(L.rh_hi[:, k], L.gate[:, k]).then_inc(L.s_rh_hi, 1)

            def update_gate(L, n, k):
                act.wait_ge(L.s_update, upto(n, k))
                act.activation(L.z[:, k], L.ps0[:, k], ACT.Sigmoid, bias=bias_z[:, k:k + 1]).then_inc(L.s_z, 1)

            def keep_gate(L, n, k):
                act.wait_ge(L.s_update, upto(n, k))
                act.activation(L.kept[:, k], L.ps0[:, k], ACT.Sigmoid, bias=neg_bias_z[:, k:k + 1],
                               scale=-1.0).then_inc(L.s_omz, 1)

            def candidate(L, n, k):
                act.wait_ge(L.s_cand, upto(n, k))
                act.activation(L.cand[:, k], L.ps1[:, k], ACT.Tanh, bias=bias_c[:, k:k + 1]).then_inc(L.s_tanh, 1)

            def feat_hi(S, v, k):
                act.wait_ge(S.s_feat, upto(v, k))
                if S is state_b and later(v):
                    act.wait_ge(back.s_base, upto(v - 1))
                copy(S.feat_hi[:, k], S.feat[:, k]).then_inc(S.s_feat_hi, 1)

            def node_hi(S, v, g, turned):
                act.wait_ge(S.s_turned, turned)
                if S is state_b and later(v):
                    act.wait_ge(back.s_mixed, upto(v - 1))
                copy(S.node_hi[:, g].rearrange("p c d -> p (c d)"), front.ps1[:, g]).then_inc(S.s_node_hi, 1)

            def graph_hi(dst, src, ready, count, g, done):
                act.wait_ge(ready, count)
                copy(dst[:, g].rearrange("p c n -> p (c n)"), src).then_inc(done, 1)

            def x1_hi(Y, q, g):
                graph_hi(Y.x_hi, Y.ps1[:, g], Y.s_x1_turned, upto(q, g), g, Y.s_x1_hi)

            def keys_hi(Y, q, g):
                graph_hi(Y.y_hi, Y.ps0[:, g], Y.s_y, upto(q, g), g, Y.s_y_hi)

            def values_hi(Y, q, g):
                graph_hi(Y.v_hi, Y.ps1[:, g], Y.s_v, upto(q, g), g, Y.s_v_hi)

            def relation_hi(Y, q, g):
                act.wait_ge(Y.s_masked, upto(q, g))
                copy(Y.rel_hi[:, g], Y.rel[:, g]).then_inc(Y.s_rel_hi, 1)

            def relation_squares(Y, q, g):
                act.wait_ge(Y.s_masked, upto(q, g))
                act.activation(Y.rel_sq[:, g], Y.rel[:, g], ACT.Square).then_inc(Y.s_rel_sq, 1)

            def squares_hi(Y, q, g):
                act.wait_ge(Y.s_sq_sum, upto(q, g))
                copy(Y.sq_hi[:, g], Y.sq_sum[:, g]).then_inc(Y.s_sq_hi, 1)

            def conv_x_hi(Y, q, j, g):
                act.wait_ge(Y.s_normed, ln(q, j + 1, g))
                copy(Y.x_hi[:, g], Y.normed[:, g]).then_inc(Y.s_x_hi, 1)

            def conv_ax_hi(Y, q, j, g):
                graph_hi(Y.y_hi, Y.ps1[:, g], Y.s_ax, conv(q, j, g), g, Y.s_ax_hi)

            def body(p, q):
                input_nodes_hi(p, 0)
                input_hi(p, 0)
                a_hi(back, q, 0)
                input_hi(p, 1)
                a_hi(back, q, 1)
                for k in range(2):
                    keep_base(back, q, k)
                for k in range(2):
                    reset_gate(back, q, k)
                rh_hi(back, q, 0)
                keep_gate(back, q, 0)
                rh_hi(back, q, 1)
                input_nodes_hi(p, 1)
                for k in range(2):
                    update_gate(back, q, k)
                keep_gate(back, q, 1)
                for k in range(2):
                    candidate(back, q, k)
                for k in range(2):
                    a_hi(front, 2 * p, k)
                for k in range(2):
                    keep_base(front, 2 * p, k)
                reset_gate(front, 2 * p, 0)
                update_gate(front, 2 * p, 0)
                reset_gate(front, 2 * p, 1)
                for k in range(2):
                    rh_hi(front, 2 * p, k)
                keep_gate(front, 2 * p, 0)
                for k in range(2):
                    x1_hi(main, q, k)
                update_gate(front, 2 * p, 1)
                keep_gate(front, 2 * p, 1)
                candidate(front, 2 * p, 0)
                for k in range(2):
                    keys_hi(main, q, k)
                feat_hi(state_f, 2 * p + 1, 0)
                candidate(front, 2 * p, 1)
                relation_squares(main, q, 0)
                relation_hi(main, q, 0)
                values_hi(main, q, 0)
                squares_hi(main, q, 0)
                for k in range(2):
                    node_hi(state_f, 2 * p + 1, k, 2 * p + k + 1)
                relation_squares(main, q, 1)
                relation_hi(main, q, 1)
                values_hi(main, q, 1)
                squares_hi(main, q, 1)
                feat_hi(state_f, 2 * p + 1, 1)
                for k in range(2):
                    a_hi(front, 2 * p + 1, k)
                conv_x_hi(main, q, 0, 0)
                for k in range(2):
                    keep_base(front, 2 * p + 1, k)
                reset_gate(front, 2 * p + 1, 0)
                conv_x_hi(main, q, 0, 1)
                reset_gate(front, 2 * p + 1, 1)
                conv_ax_hi(main, q, 0, 0)
                update_gate(front, 2 * p + 1, 0)
                rh_hi(front, 2 * p + 1, 0)
                conv_ax_hi(main, q, 0, 1)
                keep_gate(front, 2 * p + 1, 0)
                rh_hi(front, 2 * p + 1, 1)
                candidate(front, 2 * p + 1, 0)
                update_gate(front, 2 * p + 1, 1)
                conv_x_hi(main, q, 1, 0)
                keep_gate(front, 2 * p + 1, 1)
                conv_x_hi(main, q, 1, 1)
                candidate(front, 2 * p + 1, 1)
                feat_hi(state_b, p, 0)
                for k in range(2):
                    conv_ax_hi(main, q, 1, k)
                for k in range(2):
                    node_hi(state_b, p, k, 2 * p + k + 1)
                feat_hi(state_b, p, 1)

            def finish():
                for k in range(2):
                    input_nodes_hi(LAST, k)
                for k in range(2):
                    input_hi(LAST, k)
                for k in range(2):
                    a_hi(back, LAST - 1, k)
                for k in range(2):
                    a_hi(front, 2 * LAST, k)
                for k in range(2):
                    keep_base(front, 2 * LAST, k)
                for k in range(2):
                    reset_gate(front, 2 * LAST, k)
                keep_base(back, LAST - 1, 0)
                for k in range(2):
                    rh_hi(front, 2 * LAST, k)
                update_gate(front, 2 * LAST, 0)
                for k in range(2):
                    keep_gate(front, 2 * LAST, k)
                reset_gate(back, LAST - 1, 0)
                update_gate(front, 2 * LAST, 1)
                for k in range(2):
                    candidate(front, 2 * LAST, k)
                for k in range(2):
                    feat_hi(state_f, 2 * LAST + 1, k)
                for k in range(2):
                    node_hi(state_f, 2 * LAST + 1, k, 2 * LAST + k + 1)
                update_gate(back, LAST - 1, 0)
                keep_base(back, LAST - 1, 1)
                keep_base(front, 2 * LAST + 1, 0)
                reset_gate(back, LAST - 1, 1)
                keep_gate(back, LAST - 1, 0)
                for k in range(2):
                    a_hi(front, 2 * LAST + 1, k)
                rh_hi(back, LAST - 1, 0)
                update_gate(back, LAST - 1, 1)
                keep_base(front, 2 * LAST + 1, 1)
                rh_hi(back, LAST - 1, 1)
                for k in range(2):
                    reset_gate(front, 2 * LAST + 1, k)
                rh_hi(front, 2 * LAST + 1, 0)
                keep_gate(front, 2 * LAST + 1, 0)
                rh_hi(front, 2 * LAST + 1, 1)
                update_gate(front, 2 * LAST + 1, 0)
                keep_gate(front, 2 * LAST + 1, 1)
                candidate(front, 2 * LAST + 1, 0)
                update_gate(front, 2 * LAST + 1, 1)
                candidate(front, 2 * LAST + 1, 1)
                keep_gate(back, LAST - 1, 1)
                for k in range(2):
                    feat_hi(state_f, 2 * LAST + 2, k)
                for k in range(2):
                    node_hi(state_f, 2 * LAST + 2, k, 2 * LAST + k + 3)
                for k in range(2):
                    candidate(back, LAST - 1, k)
                for k in range(2):
                    a_hi(front, 2 * LAST + 2, k)
                for k in range(2):
                    keep_base(front, 2 * LAST + 2, k)
                for k in range(2):
                    reset_gate(front, 2 * LAST + 2, k)
                rh_hi(front, 2 * LAST + 2, 0)
                keep_gate(front, 2 * LAST + 2, 0)
                rh_hi(front, 2 * LAST + 2, 1)
                x1_hi(main, LAST - 1, 0)
                keep_gate(front, 2 * LAST + 2, 1)
                update_gate(front, 2 * LAST + 2, 0)
                candidate(front, 2 * LAST + 2, 0)
                update_gate(front, 2 * LAST + 2, 1)
                candidate(front, 2 * LAST + 2, 1)
                keys_hi(main, LAST - 1, 0)
                x1_hi(main, LAST - 1, 1)
                keys_hi(main, LAST - 1, 1)
                x1_hi(last_pair, 0, 0)
                for k in range(2):
                    values_hi(main, LAST - 1, k)
                relation_squares(main, LAST - 1, 0)
                keys_hi(last_pair, 0, 0)
                relation_hi(main, LAST - 1, 0)
                squares_hi(main, LAST - 1, 0)
                values_hi(last_pair, 0, 0)
                relation_squares(main, LAST - 1, 1)
                relation_hi(main, LAST - 1, 1)
                x1_hi(last_pair, 0, 1)
                relation_squares(last_pair, 0, 0)
                relation_hi(last_pair, 0, 0)
                squares_hi(last_pair, 0, 0)
                keys_hi(last_pair, 0, 1)
                squares_hi(main, LAST - 1, 1)
                relation_hi(last_pair, 0, 1)
                relation_squares(last_pair, 0, 1)
                values_hi(last_pair, 0, 1)
                squares_hi(last_pair, 0, 1)
                conv_x_hi(main, LAST - 1, 0, 0)
                conv_x_hi(last_pair, 0, 0, 0)
                conv_ax_hi(last_pair, 0, 0, 0)
                conv_ax_hi(main, LAST - 1, 0, 0)
                conv_x_hi(main, LAST - 1, 0, 1)
                conv_x_hi(last_pair, 0, 0, 1)
                conv_ax_hi(main, LAST - 1, 0, 1)
                conv_ax_hi(last_pair, 0, 0, 1)
                conv_x_hi(last_pair, 0, 1, 0)
                conv_x_hi(main, LAST - 1, 1, 0)
                conv_ax_hi(last_pair, 0, 1, 0)
                conv_ax_hi(main, LAST - 1, 1, 0)
                conv_x_hi(last_pair, 0, 1, 1)
                conv_x_hi(main, LAST - 1, 1, 1)
                conv_ax_hi(last_pair, 0, 1, 1)
                conv_ax_hi(main, LAST - 1, 1, 1)

            prep_hi(0)
            for g in range(G):
                input_nodes_hi(0, g)
            for k in range(C):
                input_hi(0, k)
            for i in (1, 2):
                prep_hi(i)
            for k in range(C):
                a_hi(front, 0, k)
            act.wait_ge(s_bias, 4)
            for k in range(C):
                keep_base(front, 0, k)
            for i in (3, 4, 5):
                prep_hi(i)
            for k in range(C):
                reset_gate(front, 0, k)
            for k in range(C):
                rh_hi(front, 0, k)
            for k in range(C):
                keep_gate(front, 0, k)
                update_gate(front, 0, k)
            for k in range(C):
                candidate(front, 0, k)
            for k in range(C):
                feat_hi(state_f, 1, k)
            for g in range(G):
                node_hi(state_f, 1, g, g + 1)
            for i in (6, 7):
                prep_hi(i)
            for k in range(C):
                keep_base(front, 1, k)
            for k in range(C):
                a_hi(front, 1, k)
            for k in range(C):
                reset_gate(front, 1, k)
            for k in range(C):
                rh_hi(front, 1, k)
            for k in range(C):
                keep_gate(front, 1, k)
                update_gate(front, 1, k)
            act.wait_ge(s_norm_full, 1)
            copy(norm_adjT.hi[:], norm_full).then_inc(s_prep_hi, 1)
            act.wait_ge(s_load["l23"], 32)
            copy(w2s.hi[:], w2_nat).then_inc(s_prep_hi, 1)
            copy(w3s.hi[:], w3s_nat).then_inc(s_prep_hi, 1)
            for k in range(C):
                candidate(front, 1, k)
            for k in range(C):
                feat_hi(state_b, 0, k)
            for g in range(G):
                node_hi(state_b, 0, g, g + 1)
            body(1, 0)
            with act.Fori(2, LAST) as p:
                body(p, p - 1)
            finish()

        @block.vector
        def _(dve):
            def full(t):
                return t.bitcast(F32)

            def prep_lo(i, src):
                dve.wait_ge(s_prep_hi, i + 1)
                m = (prepared + [w2s, w3s])[i]
                dve.tensor_tensor(m.lo[:], src, full(m.hi[:]), ALU.subtract).then_inc(s_prep_lo, 1)

            def sum_halves(w, name):
                dve.wait_ge(s_load[name], 16)
                dve.tensor_tensor(w[:, :, 0:D], w[:, :, 0:D], w[:, :, D:2 * D], ALU.add).then_inc(s_halves, 1)

            def a_lo(L, n, k):
                dve.wait_ge(L.s_a_hi, upto(n, k))
                dve.tensor_tensor(L.a_lo[:, k], L.ps1[:, k], full(L.a_hi[:, k]), ALU.subtract).then_inc(L.s_a_lo, 1)

            def reset_arg(L, n, k):
                dve.wait_ge(L.s_base_kept, upto(n, k))
                dve.wait_ge(L.s_reset, upto(n, k))
                dve.tensor_tensor(L.gate[:, k], L.ps1[:, k], L.gate[:, k], ALU.add).then_inc(L.s_reset_arg, 1)

            def reset_h(L, n, k):
                dve.wait_ge(L.state.s_feat, upto(n, k))
                dve.wait_ge(L.s_r, upto(n, k))
                dve.tensor_tensor(L.gate[:, k], L.gate[:, k], L.state.feat[:, k], ALU.mult).then_inc(L.s_rh, 1)

            def rh_lo(L, n, k):
                dve.wait_ge(L.s_rh_hi, upto(n, k))
                dve.tensor_tensor(L.rh_lo[:, k], L.gate[:, k], full(L.rh_hi[:, k]), ALU.subtract).then_inc(L.s_rh_lo, 1)

            def candidate_part(L, n, k):
                dve.wait_ge(L.s_tanh, upto(n, k))
                dve.tensor_tensor(L.cand[:, k], L.z[:, k], L.cand[:, k], ALU.mult).then_inc(L.s_zc, 1)

            def new_h(L, n, k, dst, done):
                dve.wait_ge(L.s_kept, upto(n, k))
                dve.wait_ge(L.s_zc, upto(n, k))
                dve.tensor_tensor(dst[:, k], L.kept[:, k], L.cand[:, k], ALU.add).then_inc(done, 1)

            def hand_over_h(p, k):
                if later(p):
                    dve.wait_ge(back.s_kept, upto(p - 1, k))
                new_h(front, 2 * p + 1, k, state_b.feat, state_b.s_feat)

            def feat_lo(S, v, k):
                dve.wait_ge(S.s_feat_hi, upto(v, k))
                dve.tensor_tensor(S.feat_lo[:, k], S.feat[:, k], full(S.feat_hi[:, k]),
                                  ALU.subtract).then_inc(S.s_feat_lo, 1)

            def node_lo(S, v, g):
                dve.wait_ge(S.s_node_hi, upto(v, g))
                dve.tensor_tensor(S.node_lo[:, g], front.ps1[:, g].rearrange("p (c d) -> p c d", c=C),
                                  full(S.node_hi[:, g]), ALU.subtract).then_inc(S.s_node_lo, 1)

            def stats_of(Y, q, j, g):
                dve.wait_ge(Y.s_sum, ln(q, j, g))
                for c in range(C):
                    last = dve.bn_stats(Y.stats[:, g, c], Y.summed[:, g, c])
                last.then_inc(Y.s_stats, 1)

            def moments_of(Y, q, j, g):
                dve.wait_ge(Y.s_stats, ln(q, j, g))
                dve.memset(Y.pad[:, g:g + 1], 0.0)
                for c in range(C):
                    last = dve.bn_aggr(Y.moments[:, g, c], Y.stats[:, g, c])
                last.then_inc(Y.s_moments, 1)

            def normalise(Y, q, j, g):
                dve.wait_ge(Y.s_rstd, ln(q, j, g))
                dst = Y.result if j == 3 else Y.normed
                if j == 2:
                    dve.wait_ge(Y.s_skip, conv(q, 0, g))
                if j == 3 and later(q):
                    dve.wait_ge(s_stored, 16 * q)
                for c in range(C):
                    last = dve.tensor_scalar(dst[:, g, c], Y.summed[:, g, c], Y.moments[:, g, c, 0:1],
                                             Y.rstd[:, g, c:c + 1], ALU.subtract, ALU.mult)
                last.then_inc(Y.s_normed, 1)

            def graph_bank(ps, g):
                return ps[:, g].rearrange("p (c d) -> p c d", c=C)

            def sum_gnn(Y, q, g):
                dve.wait_ge(Y.s_x, 16 * (q + Y.x_before) + 16)
                dve.wait_ge(Y.s_h3_turned, upto(q, g))
                dve.tensor_tensor(Y.summed[:, g], graph_bank(Y.ps1, g), Y.x[:, g], ALU.add).then_inc(Y.s_sum, 1)

            def sum_attended(Y, q, g):
                dve.wait_ge(Y.s_norm_inv, upto(q, g))
                dve.wait_ge(Y.s_attended, upto(q, g))
                for c in range(C):
                    last = dve.scalar_tensor_tensor(Y.summed[:, g, c], Y.ps0[:, g, c * D:(c + 1) * D],
                                                    Y.norm_inv[:, g, c:c + 1], Y.normed[:, g, c], ALU.mult, ALU.add)
                last.then_inc(Y.s_sum, 1)

            def sum_conv(Y, q, j, g):
                dve.wait_ge(Y.s_skip, conv(q, j, g))
                dve.wait_ge(Y.s_conv, conv(q, j, g))
                dve.tensor_tensor(Y.summed[:, g], graph_bank(Y.ps0, g), Y.skip[:, g], ALU.add).then_inc(Y.s_sum, 1)

            def graph_lo(lo, hi, src, ready, count, g, done):
                dve.wait_ge(ready, count)
                dve.tensor_tensor(lo[:, g], src, full(hi[:, g]), ALU.subtract).then_inc(done, 1)

            def x1_lo(Y, q, g):
                graph_lo(Y.x_lo, Y.x_hi, graph_bank(Y.ps1, g), Y.s_x1_hi, upto(q, g), g, Y.s_x1_lo)

            def keys_lo(Y, q, g):
                graph_lo(Y.y_lo, Y.y_hi, graph_bank(Y.ps0, g), Y.s_y_hi, upto(q, g), g, Y.s_y_lo)

            def values_lo(Y, q, g):
                graph_lo(Y.v_lo, Y.v_hi, graph_bank(Y.ps1, g), Y.s_v_hi, upto(q, g), g, Y.s_v_lo)

            def mask(Y, q, g):
                dve.wait_ge(Y.s_rel, upto(q, g))
                dve.tensor_tensor(Y.rel[:, g], graph_bank(Y.ps0, g), adj_nat[:], ALU.mult).then_inc(Y.s_masked, 1)

            def relation_lo(Y, q, g):
                graph_lo(Y.rel_lo, Y.rel_hi, Y.rel[:, g], Y.s_rel_hi, upto(q, g), g, Y.s_rel_lo)

            def norms(Y, q, g):
                dve.wait_ge(Y.s_norm, upto(q, g))
                dve.tensor_copy(Y.norm_sq[:, g], Y.ps1[:, g, 0:2 * C:2]).then_inc(Y.s_norm_sq, 1)

            def conv_x_lo(Y, q, j, g):
                graph_lo(Y.x_lo, Y.x_hi, Y.normed[:, g], Y.s_x_hi, conv(q, j, g), g, Y.s_x_lo)

            def conv_ax_lo(Y, q, j, g):
                graph_lo(Y.y_lo, Y.y_hi, graph_bank(Y.ps1, g), Y.s_ax_hi, conv(q, j, g), g, Y.s_ax_lo)

            def body(p, q):
                for k in range(2):
                    a_lo(back, q, k)
                for k in range(2):
                    reset_arg(back, q, k)
                for k in range(2):
                    reset_h(back, q, k)
                for k in range(2):
                    rh_lo(back, q, k)
                candidate_part(back, q, 0)
                new_h(back, q, 0, main.h3, main.s_h3)
                candidate_part(back, q, 1)
                new_h(back, q, 1, main.h3, main.s_h3)
                a_lo(front, 2 * p, 0)
                sum_gnn(main, q, 0)
                a_lo(front, 2 * p, 1)
                stats_of(main, q, 0, 0)
                sum_gnn(main, q, 1)
                moments_of(main, q, 0, 0)
                reset_arg(front, 2 * p, 0)
                stats_of(main, q, 0, 1)
                reset_arg(front, 2 * p, 1)
                reset_h(front, 2 * p, 0)
                moments_of(main, q, 0, 1)
                normalise(main, q, 0, 0)
                reset_h(front, 2 * p, 1)
                rh_lo(front, 2 * p, 0)
                normalise(main, q, 0, 1)
                rh_lo(front, 2 * p, 1)
                for k in range(2):
                    x1_lo(main, q, k)
                candidate_part(front, 2 * p, 0)
                keys_lo(main, q, 0)
                new_h(front, 2 * p, 0, state_f.feat, state_f.s_feat)
                keys_lo(main, q, 1)
                feat_lo(state_f, 2 * p + 1, 0)
                mask(main, q, 0)
                candidate_part(front, 2 * p, 1)
                new_h(front, 2 * p, 1, state_f.feat, state_f.s_feat)
                relation_lo(main, q, 0)
                mask(main, q, 1)
                values_lo(main, q, 0)
                for k in range(2):
                    node_lo(state_f, 2 * p + 1, k)
                norms(main, q, 0)
                relation_lo(main, q, 1)
                values_lo(main, q, 1)
                feat_lo(state_f, 2 * p + 1, 1)
                sum_attended(main, q, 0)
                norms(main, q, 1)
                stats_of(main, q, 1, 0)
                a_lo(front, 2 * p + 1, 0)
                moments_of(main, q, 1, 0)
                a_lo(front, 2 * p + 1, 1)
                sum_attended(main, q, 1)
                normalise(main, q, 1, 0)
                stats_of(main, q, 1, 1)
                moments_of(main, q, 1, 1)
                conv_x_lo(main, q, 0, 0)
                reset_arg(front, 2 * p + 1, 0)
                normalise(main, q, 1, 1)
                reset_arg(front, 2 * p + 1, 1)
                conv_x_lo(main, q, 0, 1)
                reset_h(front, 2 * p + 1, 0)
                conv_ax_lo(main, q, 0, 0)
                reset_h(front, 2 * p + 1, 1)
                rh_lo(front, 2 * p + 1, 0)
                conv_ax_lo(main, q, 0, 1)
                sum_conv(main, q, 0, 0)
                rh_lo(front, 2 * p + 1, 1)
                stats_of(main, q, 2, 0)
                sum_conv(main, q, 0, 1)
                moments_of(main, q, 2, 0)
                stats_of(main, q, 2, 1)
                moments_of(main, q, 2, 1)
                normalise(main, q, 2, 0)
                candidate_part(front, 2 * p + 1, 0)
                normalise(main, q, 2, 1)
                conv_x_lo(main, q, 1, 0)
                hand_over_h(p, 0)
                conv_x_lo(main, q, 1, 1)
                candidate_part(front, 2 * p + 1, 1)
                hand_over_h(p, 1)
                conv_ax_lo(main, q, 1, 0)
                feat_lo(state_b, p, 0)
                conv_ax_lo(main, q, 1, 1)
                node_lo(state_b, p, 0)
                sum_conv(main, q, 1, 0)
                node_lo(state_b, p, 1)
                stats_of(main, q, 3, 0)
                sum_conv(main, q, 1, 1)
                moments_of(main, q, 3, 0)
                stats_of(main, q, 3, 1)
                moments_of(main, q, 3, 1)
                feat_lo(state_b, p, 1)
                for k in range(2):
                    normalise(main, q, 3, k)

            def finish():
                a_lo(front, 2 * LAST, 0)
                a_lo(back, LAST - 1, 0)
                a_lo(front, 2 * LAST, 1)
                a_lo(back, LAST - 1, 1)
                for k in range(2):
                    reset_arg(front, 2 * LAST, k)
                for k in range(2):
                    reset_h(front, 2 * LAST, k)
                for k in range(2):
                    rh_lo(front, 2 * LAST, k)
                reset_arg(back, LAST - 1, 0)
                candidate_part(front, 2 * LAST, 0)
                new_h(front, 2 * LAST, 0, state_f.feat, state_f.s_feat)
                candidate_part(front, 2 * LAST, 1)
                new_h(front, 2 * LAST, 1, state_f.feat, state_f.s_feat)
                for k in range(2):
                    feat_lo(state_f, 2 * LAST + 1, k)
                for k in range(2):
                    node_lo(state_f, 2 * LAST + 1, k)
                reset_arg(back, LAST - 1, 1)
                for k in range(2):
                    reset_h(back, LAST - 1, k)
                for k in range(2):
                    a_lo(front, 2 * LAST + 1, k)
                for k in range(2):
                    reset_arg(front, 2 * LAST + 1, k)
                for k in range(2):
                    reset_h(front, 2 * LAST + 1, k)
                for k in range(2):
                    rh_lo(front, 2 * LAST + 1, k)
                for k in range(2):
                    rh_lo(back, LAST - 1, k)
                candidate_part(front, 2 * LAST + 1, 0)
                new_h(front, 2 * LAST + 1, 0, state_f.feat, state_f.s_feat)
                candidate_part(front, 2 * LAST + 1, 1)
                new_h(front, 2 * LAST + 1, 1, state_f.feat, state_f.s_feat)
                feat_lo(state_f, 2 * LAST + 2, 0)
                for k in range(2):
                    node_lo(state_f, 2 * LAST + 2, k)
                candidate_part(back, LAST - 1, 0)
                feat_lo(state_f, 2 * LAST + 2, 1)
                new_h(back, LAST - 1, 0, main.h3, main.s_h3)
                candidate_part(back, LAST - 1, 1)
                new_h(back, LAST - 1, 1, main.h3, main.s_h3)
                for k in range(2):
                    a_lo(front, 2 * LAST + 2, k)
                for k in range(2):
                    sum_gnn(main, LAST - 1, k)
                for k in range(2):
                    stats_of(main, LAST - 1, 0, k)
                for k in range(2):
                    reset_arg(front, 2 * LAST + 2, k)
                moments_of(main, LAST - 1, 0, 0)
                reset_h(front, 2 * LAST + 2, 0)
                moments_of(main, LAST - 1, 0, 1)
                reset_h(front, 2 * LAST + 2, 1)
                normalise(main, LAST - 1, 0, 0)
                for k in range(2):
                    rh_lo(front, 2 * LAST + 2, k)
                x1_lo(main, LAST - 1, 0)
                normalise(main, LAST - 1, 0, 1)
                candidate_part(front, 2 * LAST + 2, 0)
                new_h(front, 2 * LAST + 2, 0, last_pair.h3, last_pair.s_h3)
                candidate_part(front, 2 * LAST + 2, 1)
                new_h(front, 2 * LAST + 2, 1, last_pair.h3, last_pair.s_h3)
                x1_lo(main, LAST - 1, 1)
                sum_gnn(last_pair, 0, 0)
                stats_of(last_pair, 0, 0, 0)
                moments_of(last_pair, 0, 0, 0)
                keys_lo(main, LAST - 1, 0)
                sum_gnn(last_pair, 0, 1)
                normalise(last_pair, 0, 0, 0)
                keys_lo(main, LAST - 1, 1)
                stats_of(last_pair, 0, 0, 1)
                moments_of(last_pair, 0, 0, 1)
                x1_lo(last_pair, 0, 0)
                mask(main, LAST - 1, 0)
                normalise(last_pair, 0, 0, 1)
                mask(main, LAST - 1, 1)
                values_lo(main, LAST - 1, 0)
                keys_lo(last_pair, 0, 0)
                relation_lo(main, LAST - 1, 0)
                values_lo(main, LAST - 1, 1)
                mask(last_pair, 0, 0)
                values_lo(last_pair, 0, 0)
                x1_lo(last_pair, 0, 1)
                norms(main, LAST - 1, 0)
                relation_lo(last_pair, 0, 0)
                relation_lo(main, LAST - 1, 1)
                sum_attended(main, LAST - 1, 0)
                norms(last_pair, 0, 0)
                stats_of(main, LAST - 1, 1, 0)
                keys_lo(last_pair, 0, 1)
                sum_attended(last_pair, 0, 0)
                moments_of(main, LAST - 1, 1, 0)
                stats_of(last_pair, 0, 1, 0)
                mask(last_pair, 0, 1)
                moments_of(last_pair, 0, 1, 0)
                normalise(main, LAST - 1, 1, 0)
                relation_lo(last_pair, 0, 1)
                norms(main, LAST - 1, 1)
                normalise(last_pair, 0, 1, 0)
                values_lo(last_pair, 0, 1)
                sum_attended(main, LAST - 1, 1)
                conv_x_lo(main, LAST - 1, 0, 0)
                norms(last_pair, 0, 1)
                conv_x_lo(last_pair, 0, 0, 0)
                stats_of(main, LAST - 1, 1, 1)
                sum_attended(last_pair, 0, 1)
                moments_of(main, LAST - 1, 1, 1)
                stats_of(last_pair, 0, 1, 1)
                conv_ax_lo(last_pair, 0, 0, 0)
                normalise(main, LAST - 1, 1, 1)
                moments_of(last_pair, 0, 1, 1)
                conv_ax_lo(main, LAST - 1, 0, 0)
                conv_x_lo(main, LAST - 1, 0, 1)
                sum_conv(last_pair, 0, 0, 0)
                normalise(last_pair, 0, 1, 1)
                sum_conv(main, LAST - 1, 0, 0)
                stats_of(last_pair, 0, 2, 0)
                conv_x_lo(last_pair, 0, 0, 1)
                moments_of(last_pair, 0, 2, 0)
                stats_of(main, LAST - 1, 2, 0)
                conv_ax_lo(main, LAST - 1, 0, 1)
                moments_of(main, LAST - 1, 2, 0)
                normalise(last_pair, 0, 2, 0)
                conv_ax_lo(last_pair, 0, 0, 1)
                normalise(main, LAST - 1, 2, 0)
                sum_conv(main, LAST - 1, 0, 1)
                conv_x_lo(last_pair, 0, 1, 0)
                sum_conv(last_pair, 0, 0, 1)
                conv_x_lo(main, LAST - 1, 1, 0)
                stats_of(last_pair, 0, 2, 1)
                stats_of(main, LAST - 1, 2, 1)
                moments_of(last_pair, 0, 2, 1)
                conv_ax_lo(last_pair, 0, 1, 0)
                moments_of(main, LAST - 1, 2, 1)
                conv_ax_lo(main, LAST - 1, 1, 0)
                normalise(last_pair, 0, 2, 1)
                normalise(main, LAST - 1, 2, 1)
                conv_x_lo(last_pair, 0, 1, 1)
                sum_conv(last_pair, 0, 1, 0)
                conv_x_lo(main, LAST - 1, 1, 1)
                stats_of(last_pair, 0, 3, 0)
                sum_conv(main, LAST - 1, 1, 0)
                conv_ax_lo(last_pair, 0, 1, 1)
                stats_of(main, LAST - 1, 3, 0)
                moments_of(last_pair, 0, 3, 0)
                conv_ax_lo(main, LAST - 1, 1, 1)
                sum_conv(last_pair, 0, 1, 1)
                moments_of(main, LAST - 1, 3, 0)
                stats_of(last_pair, 0, 3, 1)
                sum_conv(main, LAST - 1, 1, 1)
                moments_of(last_pair, 0, 3, 1)
                stats_of(main, LAST - 1, 3, 1)
                normalise(last_pair, 0, 3, 0)
                moments_of(main, LAST - 1, 3, 1)
                normalise(last_pair, 0, 3, 1)
                for k in range(2):
                    normalise(main, LAST - 1, 3, k)

            prep_lo(0, prep_bank(0))
            for g in range(G):
                dve.wait_ge(state_f.s_node_hi, upto(0, g))
                dve.tensor_tensor(state_f.node_lo[:, g], x_front[:, g], full(state_f.node_hi[:, g]),
                                  ALU.subtract).then_inc(state_f.s_node_lo, 1)
            for k in range(C):
                dve.wait_ge(state_f.s_feat, upto(0, k))
                dve.tensor_tensor(state_f.feat_lo[:, k], state_f.feat[:, k], full(state_f.feat_hi[:, k]),
                                  ALU.subtract).then_inc(state_f.s_feat_lo, 1)
            sum_halves(w4_nat, "w4")
            prep_lo(1, prep_bank(1))
            dve.wait_ge(s_load["bias"], 16 * 5)
            dve.tensor_tensor(bias_z[:], bias_in[:, 0], bias_in[:, 1], ALU.add).then_inc(s_bias, 1)
            dve.tensor_tensor(bias_r[:], bias_in[:, 2], bias_in[:, 1], ALU.add).then_inc(s_bias, 1)
            dve.tensor_tensor(bias_c[:], bias_in[:, 3], bias_in[:, 4], ALU.add).then_inc(s_bias, 1)
            dve.wait_ge(s_bias, 3)
            dve.tensor_scalar(neg_bias_z[:], bias_z[:], -1.0, None, ALU.mult).then_inc(s_bias, 1)
            sum_halves(w3_nat, "w3")
            prep_lo(2, prep_bank(2))
            for k in range(C):
                a_lo(front, 0, k)
            sum_halves(w5_nat, "w5")
            for i in (3, 4, 5):
                prep_lo(i, prep_bank(i))
            for k in range(C):
                reset_arg(front, 0, k)
            for k in range(C):
                reset_h(front, 0, k)
            for k in range(C):
                rh_lo(front, 0, k)
            dve.tensor_reduce(deg[:], adj_nat[:], AX.X, ALU.add).then_inc(s_deg, 1)
            dve.wait_ge(s_deg, 1)
            dve.tensor_scalar(deg_floor[:], deg[:], TINY, None, ALU.max).then_inc(s_deg, 1)
            dve.tensor_scalar(deg_pos[:], deg[:], 0.0, None, ALU.is_gt).then_inc(s_deg, 1)
            dve.wait_ge(s_deg, 3)
            dve.wait_ge(s_deg_pow, 1)
            dve.tensor_tensor(deg_inv[:], deg_pow[:], deg_pos[:], ALU.mult).then_inc(s_deg, 1)
            for k in range(C):
                candidate_part(front, 0, k)
                new_h(front, 0, k, state_f.feat, state_f.s_feat)
            for k in range(C):
                feat_lo(state_f, 1, k)
            for g in range(G):
                node_lo(state_f, 1, g)
            dve.wait_ge(s_deg, 4)
            for c in range(C):
                last = dve.tensor_scalar(adj_rows[:, c], adj_nat[:, c], deg_inv[:, c:c + 1], None, ALU.mult)
            last.then_inc(s_rows, 1)
            for i in (6, 7):
                prep_lo(i, prep_bank(i))
            for k in range(C):
                a_lo(front, 1, k)
            for k in range(C):
                reset_arg(front, 1, k)
            for k in range(C):
                reset_h(front, 1, k)
            for k in range(C):
                rh_lo(front, 1, k)
            dve.wait_ge(s_prep, 9)
            for c in range(C):
                last = dve.tensor_scalar(norm_full[:, c], prep_bank(8)[:, c], deg_inv[:, c:c + 1], None, ALU.mult)
            last.then_inc(s_norm_full, 1)
            for i, src in ((8, norm_full), (9, w2_nat), (10, w3s_nat)):
                prep_lo(i, src)
            for k in range(C):
                candidate_part(front, 1, k)
                hand_over_h(0, k)
            for k in range(C):
                feat_lo(state_b, 0, k)
            for g in range(G):
                node_lo(state_b, 0, g)
            body(1, 0)
            with dve.Fori(2, LAST) as p:
                body(p, p - 1)
            finish()


_INS = ["x", "adj", "L0_gnn_w3_w", "L0_gnn_w3_b", "L0_gnn_u3_w", "L0_gnn_u3_b", "L0_gnn_w4_w", "L0_gnn_w4_b",
        "L0_gnn_w5_w", "L0_gnn_w5_b", "L0_gnn_u5_w", "L0_gnn_u5_b", "L1_gnn_Wq", "L1_gnn_Wk", "L1_gnn_Wv",
        "L2_gnn_weight", "L2_gnn_bias", "L3_gnn_weight", "L3_gnn_bias"]


def kernel(**inputs):
    import numpy as _np
    import concourse.bacc as _bacc
    from concourse.bass_utils import run_bass_kernel_spmd as _run

    nc = _bacc.Bacc("TRN2", target_bir_lowering=False, num_devices=1)
    arrays, args = {}, []
    for name in _INS:
        a = _np.ascontiguousarray(inputs[name])
        arrays[f"in_{name}"] = a
        args.append(nc.dram_tensor(f"in_{name}", a.shape, mybir.dt.from_np(a.dtype), kind="ExternalInput").ap())
    shape = inputs["x"].shape
    args.append(nc.dram_tensor("out_0", shape, F32, kind="ExternalOutput").ap())
    build(nc, *args)
    r = _run(nc, [arrays], core_ids=[0])
    return r.results[0]["out_0"]
```
